# Optimizing a Trainium2 kernel written in Bass

```python
import numpy as np
import jax
import jax.numpy as jnp

def _softmax(x, axis=-1):
    return jax.nn.softmax(x, axis=axis)

def _gelu(x):
    return jax.nn.gelu(x, approximate=True)

def _silu(x):
    return jax.nn.silu(x)

def _sigmoid(x):
    return jax.nn.sigmoid(x)

def _layernorm(x, axis=-1, eps=1e-05):
    m = jnp.mean(x, axis=axis, keepdims=True)
    v = jnp.var(x, axis=axis, keepdims=True)
    return (x - m) / jnp.sqrt(v + eps)

def _scatter_add(tgt, idx, src, axis=0):
    return tgt.at[idx].add(src)

def _segment_sum(src, seg, n):
    return jax.ops.segment_sum(src, seg, n)
kernel_name = 'mk_seq_preln_d1_jaxref_r8_7ce3b1'

def setup_inputs(seed: int=0):
    np.random.seed(seed)
    _w = jnp.asarray

    def _L0_attn_setup():
        import jax, jax.numpy as jnp
        import numpy as np
        B, T, D, H = (4, 256, 128, 16)
        HEAD_DIM = D // H
        LOCAL_WINDOW = 64

        def _rotate_half(t):
            t1, t2 = jnp.split(t, 2, axis=-1)
            return jnp.concatenate([-t2, t1], axis=-1)

        def _apply_rope(q, k):
            Tq, d = (q.shape[2], q.shape[3])
            half = d // 2
            theta = 1.0 / 10000.0 ** (jnp.arange(half, dtype=jnp.float32) / half)
            pos = jnp.arange(Tq, dtype=jnp.float32)
            freqs = pos[:, None] * theta[None, :]
            freqs = jnp.concatenate([freqs, freqs], axis=-1)
            cos = jnp.cos(freqs)[None, None]
            sin = jnp.sin(freqs)[None, None]
            q = q * cos + _rotate_half(q) * sin
            k = k * cos + _rotate_half(k) * sin
            return (q, k)
        key = jax.random.key(seed)
        k1, k2, k3 = jax.random.split(key, 3)
        x = jax.random.normal(k1, (B, T, D), dtype=jnp.float32)
        Wqkv = jax.random.normal(k2, (D, 3 * D), dtype=jnp.float32) * 0.02
        Wout = jax.random.normal(k3, (D, D), dtype=jnp.float32) * 0.02
        return {'x': x, 'Wqkv': Wqkv, 'Wout': Wout}
    _L0_attn_in = _L0_attn_setup()

    def _L0_ffn_setup():
        import jax, jax.numpy as jnp
        import numpy as np
        B, S, D = (2, 256, 128)
        E, G, K = (32, 8, 4)
        H, SH = (256, 256)
        CAP_FACTOR = 1.25

        def _l2norm(v):
            n = jnp.linalg.norm(v, axis=-1, keepdims=True)
            return v / jnp.maximum(n, 1e-12)
        key = jax.random.key(seed)
        ks = jax.random.split(key, 10)
        x = jax.random.normal(ks[0], (B, S, D), jnp.float32)
        group_centroids = jax.random.normal(ks[1], (G, D), jnp.float32) * 0.02
        expert_centroids = jax.random.normal(ks[2], (E, D), jnp.float32) * 0.02
        bias = jnp.zeros((E,), jnp.float32)
        sd_in = 1.0 / np.sqrt(D).astype(np.float32)
        sd_h = 1.0 / np.sqrt(H).astype(np.float32)
        wg = jax.random.normal(ks[3], (E, D, H), jnp.float32) * sd_in
        wu = jax.random.normal(ks[4], (E, D, H), jnp.float32) * sd_in
        wd = jax.random.normal(ks[5], (E, H, D), jnp.float32) * sd_h
        sg = jax.random.normal(ks[6], (D, SH), jnp.float32) * sd_in
        su = jax.random.normal(ks[7], (D, SH), jnp.float32) * sd_in
        sd_w = jax.random.normal(ks[8], (SH, D), jnp.float32) * sd_h
        return dict(x=x, group_centroids=group_centroids, expert_centroids=expert_centroids, bias=bias, wg=wg, wu=wu, wd=wd, sg=sg, su=su, sd=sd_w)
    _L0_ffn_in = _L0_ffn_setup()
    _d = {'L0_attn_x': _L0_attn_in['x'], 'L0_attn_Wqkv': _L0_attn_in['Wqkv'], 'L0_attn_Wout': _L0_attn_in['Wout'], 'L0_ffn_group_centroids': _L0_ffn_in['group_centroids'], 'L0_ffn_expert_centroids': _L0_ffn_in['expert_centroids'], 'L0_ffn_bias': _L0_ffn_in['bias'], 'L0_ffn_wg': _L0_ffn_in['wg'], 'L0_ffn_wu': _L0_ffn_in['wu'], 'L0_ffn_wd': _L0_ffn_in['wd'], 'L0_ffn_sg': _L0_ffn_in['sg'], 'L0_ffn_su': _L0_ffn_in['su'], 'L0_ffn_sd': _L0_ffn_in['sd']}
    _x0 = _d['L0_attn_x']
    _d['L0_attn_x'] = jax.random.normal(jax.random.fold_in(jax.random.key(seed), 1), (4, 1024, 128), dtype=_x0.dtype)
    del _x0
    return _d

def reference(L0_attn_x, L0_attn_Wqkv, L0_attn_Wout, L0_ffn_group_centroids, L0_ffn_expert_centroids, L0_ffn_bias, L0_ffn_wg, L0_ffn_wu, L0_ffn_wd, L0_ffn_sg, L0_ffn_su, L0_ffn_sd):

    def _L0_attn_ref(x, Wqkv, Wout):
        import jax, jax.numpy as jnp
        import numpy as np
        B, T, D, H = (4, 256, 128, 16)
        HEAD_DIM = D // H
        LOCAL_WINDOW = 64

        def _rotate_half(t):
            t1, t2 = jnp.split(t, 2, axis=-1)
            return jnp.concatenate([-t2, t1], axis=-1)

        def _apply_rope(q, k):
            Tq, d = (q.shape[2], q.shape[3])
            half = d // 2
            theta = 1.0 / 10000.0 ** (jnp.arange(half, dtype=jnp.float32) / half)
            pos = jnp.arange(Tq, dtype=jnp.float32)
            freqs = pos[:, None] * theta[None, :]
            freqs = jnp.concatenate([freqs, freqs], axis=-1)
            cos = jnp.cos(freqs)[None, None]
            sin = jnp.sin(freqs)[None, None]
            q = q * cos + _rotate_half(q) * sin
            k = k * cos + _rotate_half(k) * sin
            return (q, k)
        Bx, Tx, C = x.shape
        h, d, w = (H, HEAD_DIM, LOCAL_WINDOW)
        qkv = x @ Wqkv
        q, k, v = jnp.split(qkv, 3, axis=-1)
        q = q.reshape(Bx, Tx, h, d).transpose(0, 2, 1, 3)
        k = k.reshape(Bx, Tx, h, d).transpose(0, 2, 1, 3)
        v = v.reshape(Bx, Tx, h, d).transpose(0, 2, 1, 3)
        q, k = _apply_rope(q, k)
        idx = jnp.arange(Tx)
        dist = idx[None, :] - idx[:, None]
        allowed = (dist <= 0) & (dist >= -(w - 1))
        scores = jnp.einsum('bhqd,bhkd->bhqk', q, k) / jnp.sqrt(jnp.float32(d))
        scores = jnp.where(allowed[None, None], scores, -jnp.inf)
        weights = jax.nn.softmax(scores, axis=-1)
        out = jnp.einsum('bhqk,bhkd->bhqd', weights, v)
        out = out.transpose(0, 2, 1, 3).reshape(Bx, Tx, C)
        return out @ Wout

    def _L0_ffn_ref(x, group_centroids, expert_centroids, bias, wg, wu, wd, sg, su, sd):
        import jax, jax.numpy as jnp
        import numpy as np
        B, S, D = (2, 256, 128)
        E, G, K = (32, 8, 4)
        H, SH = (256, 256)
        CAP_FACTOR = 1.25

        def _l2norm(v):
            n = jnp.linalg.norm(v, axis=-1, keepdims=True)
            return v / jnp.maximum(n, 1e-12)
        b, s, d = x.shape
        xf = x.reshape(-1, d)
        N = xf.shape[0]
        shared = jax.nn.silu(xf @ sg) * (xf @ su) @ sd
        xn = _l2norm(xf)
        group_scores = xn @ _l2norm(group_centroids).T
        n_top_groups = max(1, G // 2)
        _, top_group_idx = jax.lax.top_k(group_scores, n_top_groups)
        expert_scores = xn @ _l2norm(expert_centroids).T + bias
        expert_to_group = jnp.arange(E) // (E // G)
        sel = jnp.zeros((N, G), xf.dtype).at[jnp.arange(N)[:, None], top_group_idx].set(1.0)
        group_mask = sel[:, expert_to_group]
        masked = expert_scores * group_mask + (1.0 - group_mask) * -1000000000.0
        top_scores, top_idx = jax.lax.top_k(masked, K)
        gates = jax.nn.softmax(top_scores, axis=-1)
        capacity = max(1, int(N / E * K * CAP_FACTOR))
        flat_e = top_idx.reshape(-1)
        flat_g = gates.reshape(-1)
        tok = jnp.repeat(jnp.arange(N), K)
        onehot = jax.nn.one_hot(flat_e, E, dtype=jnp.int32)
        pos = jnp.cumsum(onehot, axis=0)[jnp.arange(N * K), flat_e] - 1
        keep = pos < capacity
        e_s = jnp.where(keep, flat_e, E)
        p_s = jnp.where(keep, pos, 0)
        buf = jnp.zeros((E + 1, capacity, d), xf.dtype).at[e_s, p_s].set(xf[tok])[:E]
        h = jax.nn.silu(jnp.einsum('ecd,edh->ech', buf, wg)) * jnp.einsum('ecd,edh->ech', buf, wu)
        out_e = jnp.einsum('ech,ehd->ecd', h, wd)
        gathered = out_e[flat_e, jnp.minimum(pos, capacity - 1)]
        contrib = gathered * (flat_g * keep.astype(xf.dtype))[:, None]
        routed = jnp.zeros_like(xf).at[tok].add(contrib)
        return (shared + routed).reshape(b, s, d)
    x = L0_attn_x
    x = x + _L0_attn_ref(_layernorm(x, axis=-1), L0_attn_Wqkv, L0_attn_Wout)
    x = x + _L0_ffn_ref(_layernorm(x, axis=-1), L0_ffn_group_centroids, L0_ffn_expert_centroids, L0_ffn_bias, L0_ffn_wg, L0_ffn_wu, L0_ffn_wd, L0_ffn_sg, L0_ffn_su, L0_ffn_sd)
    return x

_drawn_inputs = setup_inputs


def setup_inputs(seed=0):
    import zlib

    import numpy as np

    out = dict(_drawn_inputs(seed))
    spreads = {'L0_ffn_bias': (0.0, 0.1)}
    factors = {}
    for name, (base, spread) in spreads.items():
        noise = np.random.default_rng([zlib.crc32(name.encode()), seed]).standard_normal(out[name].shape)
        drawn = base * np.exp(spread * noise) if base else spread * noise
        out[name] = jnp.asarray(drawn.astype(out[name].dtype))
    for name, factor in factors.items():
        out[name] = (out[name] * factor).astype(out[name].dtype)
    return out
```

```python
from collections import namedtuple
from contextlib import ExitStack

import concourse.bass as bass
from concourse import mybir

F32 = mybir.dt.float32
F32R = mybir.dt.float32r
BF16 = mybir.dt.bfloat16
U32 = mybir.dt.uint32
ALU = mybir.AluOpType
ACT = mybir.ActivationFunctionType
AX = mybir.AxisListType

P = 128
H, DH, WIN = 16, 8, 64
HALF = DH // 2
STRIP = 32
NS = P // STRIP
NG = H // NS
PEN_ROW = 3 * DH
NEG = -1e30
NE, NGR, TOPG, TOPK = 32, 8, 4, 4
EPG = NE // NGR
FF = 256
EPS = 1e-5

Tile = namedtuple("Tile", "n half b")


def tile_of(half, b):
    return Tile(2 * half + b, half, b)


def constants(N, T):
    import numpy as np

    cap = max(1, int(N / NE * TOPK * 1.25))
    p = np.arange(P)
    theta = (1.0 / np.float32(10000.0) ** (np.arange(HALF, dtype=np.float32) / np.float32(HALF))).astype(np.float32)
    pos = (np.arange(N) % T).astype(np.float32)
    freq = (pos[:, None] * theta[None, :]).astype(np.float32)
    per_tile = lambda a: a.reshape(N // P, P, HALF).transpose(1, 0, 2).reshape(P, -1)
    j = np.arange(P + WIN)
    pen = np.zeros((P, N // P), np.float32)
    pen[PEN_ROW::STRIP, T // P - 1::T // P] = NEG
    kb = np.arange(P)[None, :]
    qb = np.arange(WIN)[:, None]
    comb = np.zeros((P, P), np.float32)
    comb[:WIN] = np.where((kb > qb) & (kb <= qb + WIN), 0.0, NEG)
    head_rows = np.zeros((P, H), np.float32)
    for part in range(3):
        head_rows[WIN + part * H:WIN + (part + 1) * H] = np.eye(H)
    fields = {
        "cos": per_tile(np.cos(freq)),
        "sin": per_tile(np.sin(freq)),
        "pen": pen,
        "ident": np.eye(P),
        "before": (p[:, None] < p[None, :]),
        "maskq": np.where((j[None, :] > p[:, None]) & (j[None, :] <= p[:, None] + WIN), 0.0, NEG),
        "comb": comb,
        "head_rows": head_rows,
        "eye2": np.concatenate([np.eye(P)[:, :WIN], np.eye(P)[:, :WIN]], 1),
        "numbers": np.tile(np.arange(NE), (P, 1)),
        "pair": ((np.arange(N // P)[None, :, None] * P + p[:, None, None]) * TOPK + np.arange(TOPK)).reshape(P, -1),
    }
    at, where = 0, {}
    for name, a in fields.items():
        where[name] = (at, a.shape[1])
        at += a.shape[1]
    return np.concatenate([np.asarray(a, np.float32) for a in fields.values()], 1), where, cap


def block_kernel(nc, x, w_qkv, w_out, group_c, expert_c, bias, w_g, w_u, w_d, s_g, s_u, s_d, const, out, where, cap):
    BT, T, D = x.shape
    N = BT * T
    NT = N // P
    NSLOT = NE * cap
    ST = cap // P
    SPAN = P + WIN
    ROW = D + 1
    OOB = float(1 << 20)
    QK_SCALE = float(DH) ** -0.5
    CH = cap // 2
    assert D == P and cap % P == 0 and NT % 2 == 0 and H * DH == D

    x_v = x.rearrange("b (t p) d -> p (b t) d", p=P)
    out_v = out.rearrange("b (t p) d -> p (b t) d", p=P)
    slots_d = nc.dram_tensor("expert_slots", [NSLOT, ROW], F32, kind="Internal").ap()
    pairs_d = nc.dram_tensor("pair_results", [N * TOPK, D], F32, kind="Internal").ap()
    slots_v = slots_d.rearrange("(e p j) c -> e p (j c)", p=P, j=ST)
    pairs_v = pairs_d.rearrange("(t p k) d -> t p (k d)", p=P, k=TOPK)

    with ExitStack() as ctx:
        def sb(name, shape, dt=F32):
            return ctx.enter_context(nc.sbuf_tensor(name, shape, dt))

        def sem(name):
            return ctx.enter_context(nc.semaphore(name))

        bank = [ctx.enter_context(nc.psum_tensor(f"bank{i}", [P, 512], F32)) for i in range(8)]

        x_all = sb("x_all", [P, NT, D])
        xfT_all = sb("xfT_all", [P, N])
        gates = sb("gates", [P, NT, TOPK])
        cst = sb("cst", [P, const.shape[1]])

        def field(name):
            at, n = where[name]
            return cst[:, at:at + n]

        cos = field("cos").rearrange("p (t i) -> p t i", i=HALF)
        sin = field("sin").rearrange("p (t i) -> p t i", i=HALF)
        pen = field("pen")
        ident = field("ident")
        numbers = field("numbers")
        pair = field("pair").rearrange("p (t k) -> p t k", k=TOPK)

        wqkv = sb("wqkv", [P, 3 * D])
        wop = sb("wop", [P, D])
        ident_b = sb("ident_b", [P, P], BF16)
        before_b = sb("before_b", [P, P], BF16)
        ones_b = sb("ones_b", [P, P], BF16)
        maskq_b = sb("maskq_b", [P, SPAN], BF16)
        comb_st = sb("comb_st", [P, H, P], BF16)
        comb_mv = sb("comb_mv", [P, 2, P], BF16)
        cent = sb("cent", [NGR + NE, D])
        cent_sq = sb("cent_sq", [NGR + NE, D])
        cent_n = sb("cent_n", [NGR + NE, 4])
        centT = sb("centT", [P, NGR + NE])
        bias_b = sb("bias_b", [P, NE])
        mhalf = sb("mhalf", [P, 4])
        st1 = sb("st1", [P, 6])
        st2 = sb("st2", [P, 6])
        mv1 = sb("mv1", [P, 2, 2])
        mv2 = sb("mv2", [P, 2, 2])
        pin = sb("pin", [P, 2, 3])
        pout = sb("pout", [P, 2, 3])
        ve = sb("ve", [P, 2])
        xn = sb("xn", [P, 2, D])
        xnT = sb("xnT", [P, 2, P])
        ra = sb("ra", [P, 2 * D])
        rb = sb("rb", [P, 2 * D])
        rr = sb("rr", [P, 2, 2 * D])
        qk = sb("qk", [P, 2, 2, H, STRIP])
        qT = sb("qT", [P, 2, NG, P], F32R)
        kT = sb("kT", [P, 2, NG, SPAN], F32R)
        v_cur = sb("v_cur", [P, 2, H, DH + 1])
        v_mix = sb("v_mix", [P, 2, H, DH + 1])
        mx = sb("mx", [P, 2, H])
        nm = sb("nm", [P, H])
        mp = sb("mp", [P, 2, 3, H], BF16)
        pt = sb("pt", [P, 2, NS, 512])
        rec = sb("rec", [P, 2, H])
        on = sb("on", [P, 2, 2, 64])
        oT = sb("oT", [P, 2, P])
        xfe = sb("xfe", [P, 2, TOPK, ROW])
        xfT = sb("xfT", [P, 2, P])
        sc = sb("sc", [P, NGR + NE])
        es = sb("es", [P, NE])
        es2 = sb("es2", [P, NE])
        gm8 = sb("gm8", [P, 8])
        gi8 = sb("gi8", [P, 8], U32)
        geq = sb("geq", [P, NGR, TOPG])
        gsel = sb("gsel", [P, NGR])
        gpen = sb("gpen", [P, NGR])
        em8 = sb("em8", [P, 8])
        ei8 = sb("ei8", [P, 8], U32)
        ed4 = sb("ed4", [P, 2, TOPK])
        ex4 = sb("ex4", [P, 2, TOPK])
        exs = sb("exs", [P, 2, 1])
        exr = sb("exr", [P, 1])
        oh = sb("oh", [P, TOPK, NE])
        msel = sb("msel", [P, 2, NE], BF16)
        macc = sb("macc", [P, 2, NE], BF16)
        ohp = sb("ohp", [P, TOPK, NE])
        posk = sb("posk", [P, TOPK])
        keep = sb("keep", [P, TOPK])
        slotf = sb("slotf", [P, TOPK])
        slotf2 = sb("slotf2", [P, TOPK])
        sidx = sb("sidx", [P, 2, TOPK], U32)
        sgw = sb("sgw", [P, FF])
        suw = sb("suw", [P, FF])
        sdw = sb("sdw", [P, 2, D])
        wgu = sb("wgu", [P, 2, 2, FF])
        wdn = sb("wdn", [P, 2, 2, D])
        sact = sb("sact", [P, 2, 2, 512])
        fill = sb("fill", [P, ST, ROW])
        xg = sb("xg", [P, 2, ST, ROW])
        xgT = sb("xgT", [P, 2, cap])
        hact = sb("hact", [P, 2, 2, cap])
        yout = sb("yout", [P, 2, ST, D])
        yidx = sb("yidx", [P, 2, ST], U32)
        rload = sb("rload", [P, 4, TOPK, D])

        names = """const_loaded x_loaded w_loaded cent_loaded fill_done zero_done filled zeroed
        cent_sum cent_len cent_unit centT_done centT_evac casts
        ln1 ln2 pow_done xn_ready xnT_done xnT_evac qkv_done rope_ab rope_r v_evac
        v_prev split_hi split_lo qkT_done qT_evac kT_evac k_prev p1_scores p1_reduced negm mT_done mT_evac
        p2_scores exp_done pv_done recip onorm oT_done oT_evac wout_done x1_ready xf_ready xfe_id
        xfT_done xfT_evac xfT_kept router_done sc_ready route gate_exp gate_done sel_ready acc_ready pos_done
        pos_read slots slot_ready sh_gu sh_act sh_mul sh_down sh_added
        xgT_done xgT_evac gu_done h_act h_mul down_done y_evac yidx_ready comb_step stored""".split()
        S = namedtuple("Semaphores", names)(*[sem(n) for n in names])
        dispatched = [sem(f"dispatched{b}") for b in range(2)]
        wgu_arrived = [sem(f"wgu_arrived{b}") for b in range(2)]
        wdn_arrived = [sem(f"wdn_arrived{b}") for b in range(2)]
        xg_arrived = [sem(f"xg_arrived{b}") for b in range(2)]
        y_sent = [sem(f"y_sent{b}") for b in range(2)]
        r_arrived = [sem(f"r_arrived{b}") for b in range(4)]

        def wait(eng, s, value):
            if not (isinstance(value, int) and value < 1):
                eng.wait_ge(s, value)

        def hold(eng):
            eng.nop(nofuse=True)

        def attention_steps(eng, step):
            FIRST = 5
            LAST = FIRST + (NT - FIRST) // 2 * 2

            def straight(tau):
                step(tau, *[tile_of((tau - k) // 2, (tau - k) % 2) if 0 <= tau - k < NT else None
                            for k in range(-1, 4)])

            for tau in range(-1, FIRST):
                straight(tau)
            with eng.Fori(0, (LAST - FIRST) // 2) as i:
                for c in range(2):
                    step(2 * i + (FIRST + c), *[tile_of(i + (FIRST + c - k) // 2, (FIRST + c - k) % 2)
                                                for k in range(-1, 4)])
            for tau in range(LAST, NT + 3):
                straight(tau)

        def lagged_steps(eng, step, count, ahead):
            FIRST = 3
            LAST = FIRST + (count - 1 - FIRST) // 2 * 2
            lags = range(-1 if ahead else 0, 2)

            def straight(n):
                step(*[tile_of((n - k) // 2, (n - k) % 2) if 0 <= n - k < count else None for k in lags])

            for n in range(-1 if ahead else 0, FIRST):
                straight(n)
            with eng.Fori(0, (LAST - FIRST) // 2) as i:
                for c in range(2):
                    step(*[tile_of(i + (FIRST + c - k) // 2, (FIRST + c - k) % 2) for k in lags])
            for n in range(LAST, count + 1):
                straight(n)

        block = ctx.enter_context(nc.Block())

        @block.sync
        def _(sp):
            sp.dma_start(cst[:, :], const).then_inc(S.const_loaded, 16)
            sp.dma_start(x_all[:, :, :], x_v).then_inc(S.x_loaded, 16)

            def load_wgu(e, c):
                sp.dma_start(wgu[:, c, 0], w_g[e]).then_inc(wgu_arrived[c], 16)
                sp.dma_start(wgu[:, c, 1], w_u[e]).then_inc(wgu_arrived[c], 16)

            def load_wdn(e, c):
                sp.dma_start(wdn[:, c], w_d[e].rearrange("(h p) n -> p h n", p=P)).then_inc(wdn_arrived[c], 16)

            def load_slots(e, c):
                sp.dma_start(xg[:, c].rearrange("p j c -> p (j c)"), slots_v[e]).then_inc(xg_arrived[c], 16)

            for e in range(2):
                load_wgu(e, e)
                load_wdn(e, e)
            sp.wait_ge(S.fill_done, 2)
            with sp.Fori(0, NE) as e:
                sp.dma_start(slots_v[e], fill[:, :, :].rearrange("p j c -> p (j c)")).then_inc(S.filled, 16)
            sp.wait_ge(S.zero_done, 1)
            with sp.Fori(0, NT) as t:
                sp.dma_start(pairs_v[t], rload[:, 0].rearrange("p k d -> p (k d)")).then_inc(S.zeroed, 16)

            for b in range(2):
                sp.wait_ge(dispatched[b], 16 * TOPK * (NT // 2))
            for e in range(2):
                load_slots(e, e)
            with sp.Fori(0, (NE - 2) // 2) as i:
                for c in range(2):
                    e = 2 * i + (2 + c)
                    sp.wait_ge(S.xgT_done, 2 * (e - 1))
                    sp.wait_ge(S.yidx_ready, e - 1)
                    load_slots(e, c)
                    sp.wait_ge(S.gu_done, 8 * (e - 1))
                    load_wgu(e, c)
                    sp.wait_ge(S.down_done, e - 1)
                    load_wdn(e, c)

            for b in range(2):
                sp.wait_ge(y_sent[b], 16 * ST * (NE // 2))
            sp.wait_ge(S.zeroed, 16 * NT)
            for c in range(4):
                sp.dma_start(rload[:, c].rearrange("p k d -> p (k d)"), pairs_v[c]).then_inc(r_arrived[c], 16)
            with sp.Fori(0, NT // 4 - 1) as i:
                for c in range(4):
                    sp.wait_ge(S.comb_step, TOPK * (4 * i + (c + 1)))
                    sp.dma_start(rload[:, c].rearrange("p k d -> p (k d)"), pairs_v[4 * i + (c + 4)])\
                      .then_inc(r_arrived[c], 16)

        @block.gpsimd
        def _(pool):
            g = nc.gpsimd
            g.memset(mhalf[:, :], -0.5).then_inc(S.cent_len, 1)
            g.memset(fill[:, :, 0:D], 0.0).then_inc(S.fill_done, 1)
            g.memset(fill[:, :, D:ROW], OOB).then_inc(S.fill_done, 1)
            g.memset(rload[:, 0], 0.0).then_inc(S.zero_done, 1)
            pool.wait_ge(S.cent_sum, 1)
            pool.wait_ge(S.cent_len, 1)
            g.tensor_scalar(cent_n[:, 1:2], cent_n[:, 0:1], 1e-24, None, ALU.max).then_inc(S.cent_len, 1)
            pool.wait_ge(S.cent_len, 2)
            g.tensor_tensor(cent_n[:, 2:3], cent_n[:, 1:2], mhalf[0:NGR + NE, 0:1], ALU.pow).then_inc(S.cent_len, 1)

            def step(tau, tn, tf, tp, tw, tr):
                if tf is not None:
                    b = tf.b
                    r = rr[:, b].rearrange("p (w h d) -> p w h d", w=2, h=H)
                    pool.wait_ge(S.rope_ab, 3 * tf.n + 3)
                    wait(pool, S.split_hi, 2 * (tf.n - 1))
                    wait(pool, S.split_lo, 2 * (tf.n - 1))
                    g.tensor_tensor(rr[:, b], ra[:, :], rb[:, :], ALU.add).then_inc(S.rope_r, 1)
                if tr is not None:
                    pool.wait_ge(S.xfT_evac, tr.n + 1)
                    hold(pool)
                    g.tensor_copy(xfT_all[:, bass.ts(tr.n, P)], xfT[:, tr.b]).then_inc(S.xfT_kept, 1)
                if tf is not None:
                    pool.wait_ge(S.split_hi, 2 * tf.n + 2)
                    g.tensor_tensor(qk[:, b, 0, :, 2 * DH:3 * DH], r[:, 0], qk[:, b, 0, :, 0:DH],
                                    ALU.subtract).then_inc(S.split_lo, 1)
                    g.tensor_tensor(qk[:, b, 1, :, DH:2 * DH], r[:, 1], qk[:, b, 1, :, 0:DH],
                                    ALU.subtract).then_inc(S.split_lo, 1)
                if tw is not None or tn is not None:
                    lo, hi = (0 if tn is not None else 1), (3 if tw is not None else 1)
                    c = tn.b if tn is not None else 1 - tw.b
                    if tn is not None:
                        pool.wait_ge(S.ln1, 3 * tn.n + 3)
                    if tw is not None:
                        pool.wait_ge(S.ln2, 6 * tw.n + 6)
                    if isinstance(tau, int) and tau == -1:
                        pool.wait_ge(S.cent_len, 1)
                    g.tensor_tensor(pout[:, c, lo:hi], pin[:, c, lo:hi], mhalf[:, lo:hi], ALU.pow)\
                     .then_inc(S.pow_done, 1)
                if tr is not None:
                    if isinstance(tr.n, int) and tr.n == 0:
                        pool.wait_ge(S.filled, 16 * NE)
                    pool.wait_ge(S.slot_ready, tr.n + 1)
                    pool.wait_ge(S.xfe_id, tr.n + 1)
                    pool.wait_ge(S.xf_ready, tr.n + 1)
                    hold(pool)
                    for k in range(TOPK):
                        g.indirect_dma_start(
                            out=slots_d, out_offset=bass.IndirectOffsetOnAxis(ap=sidx[:, tr.b, k:k + 1], axis=0),
                            in_=xfe[:, tr.b, k, :], in_offset=None, bounds_check=NSLOT - 1,
                            oob_is_err=False).then_inc(dispatched[tr.b], 16)
                if tw is not None:
                    wait(pool, dispatched[tw.b], 16 * TOPK * tw.half)
                    hold(pool)
                    g.tensor_copy(xfe[:, tw.b, :, D:ROW], pair[:, bass.ds(tw.n, 1), :].rearrange("p o k -> p k o"))\
                     .then_inc(S.xfe_id, 1)

            attention_steps(pool, step)

            pool.wait_ge(S.zeroed, 16 * NT)
            with pool.Fori(0, NE // 2) as i:
                for c in range(2):
                    e = 2 * i + c
                    pool.wait_ge(S.yidx_ready, e + 1)
                    pool.wait_ge(S.y_evac, 2 * e + 2)
                    hold(pool)
                    for j in range(ST):
                        g.indirect_dma_start(
                            out=pairs_d, out_offset=bass.IndirectOffsetOnAxis(ap=yidx[:, c, j:j + 1], axis=0),
                            in_=yout[:, c, j, :], in_offset=None, bounds_check=N * TOPK - 1,
                            oob_is_err=False).then_inc(y_sent[c], 16)

        @block.scalar
        def _(act):
            a = nc.scalar
            act.dma_start(cent[0:NGR, :], group_c).then_inc(S.cent_loaded, 16)
            act.dma_start(cent[NGR:NGR + NE, :], expert_c).then_inc(S.cent_loaded, 16)
            act.dma_start(wqkv[:, :], w_qkv).then_inc(S.w_loaded, 16)
            wo = w_out.rearrange("(pp par s d) n -> par s pp d n", pp=2, par=2, s=NS, d=DH)
            for par in range(2):
                for s in range(NS):
                    for pp in range(2):
                        r0 = par * WIN + s * 2 * DH + pp * DH
                        act.dma_start(wop[r0:r0 + DH, :], wo[par, s, pp]).then_inc(S.w_loaded, 16)
            act.dma_start(bias_b[:, :], bias.rearrange("(o e) -> o e", o=1).broadcast_to([P, NE]))\
               .then_inc(S.w_loaded, 16)
            act.dma_start(sgw[:, :], s_g).then_inc(S.w_loaded, 16)
            act.dma_start(suw[:, :], s_u).then_inc(S.w_loaded, 16)
            act.dma_start(sdw[:, :, :], s_d.rearrange("(c p) n -> p c n", c=2)).then_inc(S.w_loaded, 16)
            act.wait_ge(S.cent_loaded, 32)
            a.activation(cent_sq[:, :], cent[:, :], ACT.Square, accum_out=cent_n[:, 0:1]).then_inc(S.cent_sum, 1)

            def step(tau, tn, tf, tp, tw, tr):
                if tw is not None:
                    act.wait_ge(S.oT_done, tw.n + 1)
                    wait(act, S.wout_done, tw.n - 1)
                    a.copy(oT[:, tw.b], bank[4][:, 0:P]).then_inc(S.oT_evac, 1)
                if tf is not None:
                    act.wait_ge(S.xnT_done, tf.n + 1)
                    wait(act, S.qkv_done, tf.n - 1)
                    a.copy(xnT[:, tf.b], bank[5][:, 0:P]).then_inc(S.xnT_evac, 1)
                if tr is not None:
                    act.wait_ge(S.xfT_done, tr.n + 1)
                    wait(act, S.router_done, tr.n - 1)
                    wait(act, S.xfT_kept, tr.n - 1)
                    a.copy(xfT[:, tr.b], bank[2][:, 0:P]).then_inc(S.xfT_evac, 1)
                if tf is not None:
                    b = tf.b
                    v = bank[4][:, 2 * D:3 * D].rearrange("p (h d) -> p h d", h=H)
                    act.wait_ge(S.rope_ab, 3 * tf.n + 3)
                    wait(act, S.pv_done, tf.n - 1)
                    a.copy(v_cur[:, b, :, 0:DH], v).then_inc(S.v_evac, 1)
                    a.copy(v_mix[WIN:P, b, :, 0:DH], v[0:WIN]).then_inc(S.v_evac, 1)
                    act.wait_ge(S.rope_r, tf.n + 1)
                    wait(act, S.qkT_done, 2 * (tf.n - 1))
                    wait(act, S.split_lo, 2 * (tf.n - 1))
                    r = rr[:, b].rearrange("p (w h d) -> p w h d", w=2, h=H)
                    qd = qk[:, b, 0, :, 0:2 * DH].rearrange("p h (c d) -> p h c d", c=2).bitcast(F32R)
                    kd = qk[:, b, 1].rearrange("p h (c d) -> p h c d", c=4)[:, :, 0:3:2, :].bitcast(F32R)
                    a.copy(qd, r[:, 0].unsqueeze(2).broadcast_to([P, H, 2, DH])).then_inc(S.split_hi, 1)
                    a.copy(kd, r[:, 1].unsqueeze(2).broadcast_to([P, H, 2, DH])).then_inc(S.split_hi, 1)
                if tp is not None:
                    wait(act, S.pv_done, tp.n - 1)
                    for s in range(NS):
                        act.wait_ge(S.p2_scores, NS * tp.n + (s + 1))
                        a.activation(pt[:, tp.b, s].rearrange("p (hb g q) -> p g hb q", hb=2, g=NG),
                                     bank[2 + s % 2][:, :].rearrange("p (g hb q) -> p g hb q", g=NG, hb=2),
                                     ACT.Exp, scale=QK_SCALE).then_inc(S.exp_done, 1)
                if tf is not None:
                    wait(act, S.p2_scores, NS * (tf.n - 1))
                    act.wait_ge(S.qkT_done, 2 * tf.n + 1)
                    a.copy(qT[:, b], bank[5][:, :].rearrange("p (g t) -> p g t", g=NG)).then_inc(S.qT_evac, 1)
                    act.wait_ge(S.qkT_done, 2 * tf.n + 2)
                    a.copy(kT[:, b, :, WIN:SPAN], bank[6][:, :].rearrange("p (g t) -> p g t", g=NG))\
                     .then_inc(S.kT_evac, 1)
                    wait(act, S.pv_done, tf.n)
                    a.copy(v_mix[0:WIN, 1 - b, :, 0:DH], v[WIN:P]).then_inc(S.v_prev, 1)
                if tr is not None:
                    act.wait_ge(S.route, 12 * tr.n + 10)
                    wait(act, S.gate_done, 2 * (tr.n - 1))
                    a.activation(ex4[:, tr.b], ed4[:, tr.b], ACT.Exp, accum_out=exs[:, tr.b]).then_inc(S.gate_exp, 1)

            attention_steps(act, step)

            def shared_step(m, _):
                if m is not None:
                    for h in range(2):
                        act.wait_ge(S.sh_gu, 4 * m.n + (2 * h + 1))
                        wait(act, S.sh_down, m.n - 1)
                        a.activation(sact[:, m.b, h], bank[h][:, :], ACT.Silu).then_inc(S.sh_act, 1)

            lagged_steps(act, shared_step, N // 512, False)

            def expert_step(_, e, ed):
                def silu(ch):
                    for h in range(2):
                        act.wait_ge(S.gu_done, 8 * e.n + (4 * ch + 2 * h + 1))
                        a.activation(hact[:, e.b, h, ch * CH:(ch + 1) * CH], bank[2 + h][:, 0:CH], ACT.Silu)\
                         .then_inc(S.h_act, 1)

                if e is not None:
                    wait(act, S.down_done, e.n - 1)
                    silu(0)
                if ed is not None:
                    act.wait_ge(S.down_done, ed.n + 1)
                    wait(act, y_sent[ed.b], 16 * ST * ed.half)
                    a.copy(yout[:, ed.b, 0:4], bank[6][:, :].rearrange("p (j d) -> p j d", d=D))\
                     .then_inc(S.y_evac, 1)
                    a.copy(yout[:, ed.b, 4:ST], bank[7][:, 0:D].rearrange("p (j d) -> p j d", d=D))\
                     .then_inc(S.y_evac, 1)
                if e is not None:
                    silu(1)

            lagged_steps(act, expert_step, NE, True)

            with act.Fori(0, NT) as t:
                act.wait_ge(S.comb_step, TOPK * (t + 1))
                act.dma_start(out_v[:, bass.ds(t, 1), :], x_all[:, bass.ds(t, 1), :]).then_inc(S.stored, 16)
            act.wait_ge(S.stored, 16 * NT)

        @block.tensor
        def _(pe):
            mm = nc.tensor.matmul
            pe.wait_ge(S.casts, 16)
            pe.wait_ge(S.cent_unit, 1)
            nc.tensor.transpose(bank[0][:, 0:NGR + NE], cent_sq[:, :], ident[0:NGR + NE, 0:NGR + NE])\
              .then_inc(S.centT_done, 1)
            pe.wait_ge(S.w_loaded, 16 * 21)
            pe.wait_ge(S.centT_evac, 1)

            def step(tau, tn, tf, tp, tw, tr):
                def first_scores(u):
                    s, g2 = u % NS, u // NS
                    bk = bank[u % 2][:, 0:2 * SPAN]
                    wait(pe, S.p1_reduced, 8 * tp.n + (u - 1) if not isinstance(tp.n, int) or tp.n else u - 1)
                    mm(bk.rearrange("p (c j) -> p c j", c=2), ident_b[:, :],
                       maskq_b[:, :].unsqueeze(1).broadcast_to([P, 2, SPAN]), start=True, stop=False,
                       skip_group_check=True)
                    rows = slice(STRIP * s, STRIP * (s + 1))
                    for c in range(2):
                        last = mm(bk[:, c * SPAN:(c + 1) * SPAN], qT[rows, tp.b, 2 * g2 + c, :],
                                  kT[rows, tp.b, 2 * g2 + c, :], start=False, stop=(c == 1),
                                  skip_group_check=True)
                    last.then_inc(S.p1_scores, 1)

                def second_scores(s):
                    bk = bank[2 + s % 2]
                    wait(pe, S.exp_done, NS * tp.n + (s - 1) if not isinstance(tp.n, int) or tp.n else s - 1)
                    for g in range(NG):
                        mm(bk[:, g * P:(g + 1) * P], comb_st[0:WIN + 3 * H, NS * g + s, :],
                           comb_mv[0:WIN + 3 * H, tp.b, :], start=(g == 0), stop=False, skip_group_check=True)
                    rows = slice(STRIP * s, STRIP * (s + 1))
                    for g in range(NG):
                        for hb in range(2):
                            at = g * P + hb * WIN
                            last = mm(bk[:, at:at + WIN], kT[rows, tp.b, g, hb * WIN:hb * WIN + P],
                                      qT[rows, tp.b, g, hb * WIN:(hb + 1) * WIN], start=False,
                                      stop=(g == NG - 1 and hb == 1), skip_group_check=True)
                    last.then_inc(S.p2_scores, 1)

                if tp is not None:
                    pe.wait_ge(S.qT_evac, tp.n + 1)
                    pe.wait_ge(S.kT_evac, tp.n + 1)
                    wait(pe, S.k_prev, tp.n)
                    first_scores(0)
                    first_scores(1)
                if tw is not None:
                    pe.wait_ge(S.onorm, 2 * tw.n + 2)
                    wait(pe, S.v_prev, min(tw.n + 2, NT) if isinstance(tw.n, int) else tw.n + 2)
                    hold(pe)
                    for hb in range(2):
                        for par in range(2):
                            rows = slice(WIN * par, WIN * (par + 1))
                            last = mm(bank[4][rows, hb * WIN:(hb + 1) * WIN], on[rows, tw.b, hb, :],
                                      ident[rows, rows], start=True, stop=True)
                    last.then_inc(S.oT_done, 1)
                if tp is not None:
                    first_scores(2)
                    first_scores(3)
                if tf is not None:
                    pe.wait_ge(S.xn_ready, tf.n + 1)
                    wait(pe, S.qT_evac, tf.n)
                    nc.tensor.transpose(bank[5][:, 0:P], xn[:, tf.b], ident[:, :]).then_inc(S.xnT_done, 1)
                if tp is not None:
                    first_scores(4)
                    first_scores(5)
                if tw is not None:
                    pe.wait_ge(S.oT_evac, tw.n + 1)
                    mm(bank[7][:, 3 * P:4 * P], oT[:, tw.b], wop[:, :], start=True, stop=True)\
                      .then_inc(S.wout_done, 1)
                if tp is not None:
                    first_scores(6)
                    first_scores(7)
                if tf is not None:
                    pe.wait_ge(S.xnT_evac, tf.n + 1)
                    wait(pe, S.v_prev, tf.n)
                    wait(pe, S.oT_evac, tf.n - 1)
                    mm(bank[4][:, 0:3 * D], xnT[:, tf.b], wqkv[:, :], start=True, stop=True).then_inc(S.qkv_done, 1)
                if tr is not None:
                    pe.wait_ge(S.xf_ready, tr.n + 1)
                    pe.wait_ge(S.exp_done, NS * min(tr.n + 2, NT) if isinstance(tr.n, int) else NS * (tr.n + 2))
                    wait(pe, S.pos_read, tr.n)
                    nc.tensor.transpose(bank[2][:, 0:P], xfe[:, tr.b, 0, 0:D], ident[:, :]).then_inc(S.xfT_done, 1)
                    pe.wait_ge(S.xfT_evac, tr.n + 1)
                    mm(bank[3][:, 0:NGR + NE], xfT[:, tr.b], centT[:, :], start=True, stop=True)\
                      .then_inc(S.router_done, 1)
                if tp is not None:
                    pe.wait_ge(S.negm, 4 * tp.n + 4)
                    pe.wait_ge(S.kT_evac, tp.n + 1)
                    hold(pe)
                    nc.tensor.transpose(bank[6][:, :].bitcast(BF16)[0:3 * H, 0:P],
                                        mp[:, tp.b].rearrange("p c h -> p (c h)"), ident_b[:, :])\
                      .then_inc(S.mT_done, 1)
                    pe.wait_ge(S.mT_evac, tp.n + 1)
                    if tr is not None:
                        pe.wait_ge(S.xfT_evac, tr.n + 1)
                        pe.wait_ge(S.sc_ready, tr.n + 1)
                    for s in range(NS):
                        second_scores(s)
                if tf is not None:
                    pe.wait_ge(S.split_hi, 2 * tf.n + 2)
                    pe.wait_ge(S.split_lo, 2 * tf.n + 2)
                    for w in range(2):
                        for gg in range(NG):
                            last = nc.tensor.transpose(
                                bank[5 + w][:, gg * P:(gg + 1) * P],
                                qk[:, tf.b, w, NS * gg:NS * (gg + 1), :].rearrange("p h d -> p (h d)"), ident[:, :])
                        last.then_inc(S.qkT_done, 1)
                if tp is not None:
                    pe.wait_ge(S.exp_done, NS * tp.n + NS)
                    pe.wait_ge(S.v_evac, 2 * tp.n + 2)
                    wait(pe, S.v_prev, tp.n)
                    wait(pe, S.x1_ready, tp.n)
                    for hb in range(2):
                        vals = (v_cur if hb else v_mix)[:, tp.b].rearrange("p (pp c s) d -> p s pp c d", pp=2, c=2)
                        for s in range(NS):
                            for pp in range(2):
                                at = ((hb * NS + s) * 2 + pp) * 2 * (DH + 1)
                                last = mm(bank[7][:, at:at + 2 * (DH + 1)], pt[:, tp.b, s, (2 * hb + pp) * P:(2 * hb + pp + 1) * P],
                                          vals[:, s, pp], start=True, stop=True)
                    last.then_inc(S.pv_done, 1)
                if tr is not None:
                    pe.wait_ge(S.sel_ready, tr.n + 1)
                    wait(pe, S.acc_ready, tr.n)
                    if tp is not None:
                        pe.wait_ge(S.exp_done, NS * tp.n + NS)
                    pe.wait_ge(S.sc_ready, tr.n + 1)
                    mm(bank[3][:, P:P + NE], before_b[:, :], msel[:, tr.b], start=True, stop=False)
                    mm(bank[3][:, P:P + NE], ones_b[:, :], macc[:, tr.b], start=False, stop=True)\
                      .then_inc(S.pos_done, 1)

            attention_steps(pe, step)

            pe.wait_ge(S.p1_reduced, 8 * NT)
            pe.wait_ge(S.pos_read, NT)
            pe.wait_ge(S.xfT_kept, NT)
            pe.wait_ge(S.x1_ready, NT)

            def shared_step(m, md):
                if m is not None:
                    for h in range(2):
                        cols = slice(h * P, (h + 1) * P)
                        wait(pe, S.sh_act, 2 * m.n + (h - 1) if not isinstance(m.n, int) or m.n else 0)
                        mm(bank[h][:, :], sgw[:, cols], xfT_all[:, bass.ts(m.n, 512)], start=True, stop=True)\
                          .then_inc(S.sh_gu, 1)
                        wait(pe, S.sh_mul, 2 * m.n + (h - 1) if not isinstance(m.n, int) or m.n else 0)
                        mm(bank[2 + h][:, :], suw[:, cols], xfT_all[:, bass.ts(m.n, 512)], start=True, stop=True)\
                          .then_inc(S.sh_gu, 1)
                if md is not None:
                    pe.wait_ge(S.sh_mul, 2 * md.n + 2)
                    wait(pe, S.sh_added, md.n - 1)
                    for j in range(4):
                        for h in range(2):
                            last = mm(bank[4 + md.b][:, j * D:(j + 1) * D], sact[:, md.b, h, j * P:(j + 1) * P],
                                      sdw[:, h, :], start=(h == 0), stop=(h == 1))
                    last.then_inc(S.sh_down, 1)

            lagged_steps(pe, shared_step, N // 512, False)
            pe.wait_ge(S.sh_added, N // 512)

            def expert_step(en, e, ed):
                def gate_up(ch):
                    for h in range(2):
                        for w in range(2):
                            wait(pe, (S.h_act, S.h_mul)[w],
                                 4 * e.n + (2 * ch + h - 1) if not isinstance(e.n, int) or e.n else 2 * ch + h - 1)
                            mm(bank[2 + 2 * w + h][:, 0:CH], wgu[:, e.b, w, h * P:(h + 1) * P],
                               xgT[:, e.b, ch * CH:(ch + 1) * CH], start=True, stop=True).then_inc(S.gu_done, 1)

                if e is not None:
                    pe.wait_ge(wgu_arrived[e.b], 32 * (e.half + 1))
                    pe.wait_ge(S.xgT_evac, 2 * e.n + 2)
                    gate_up(0)
                if ed is not None:
                    pe.wait_ge(wdn_arrived[ed.b], 16 * (ed.half + 1))
                    pe.wait_ge(S.h_mul, 4 * ed.n + 4)
                    wait(pe, S.y_evac, 2 * ed.n)
                    for j in range(ST):
                        for h in range(2):
                            last = mm(bank[6 + j // 4][:, j % 4 * D:(j % 4 + 1) * D],
                                      hact[:, ed.b, h, j * P:(j + 1) * P], wdn[:, ed.b, h, :],
                                      start=(h == 0), stop=(h == 1))
                    last.then_inc(S.down_done, 1)
                if e is not None:
                    gate_up(1)
                if en is not None:
                    pe.wait_ge(xg_arrived[en.b], 16 * (en.half + 1))
                    wait(pe, S.xgT_evac, 2 * en.n)
                    for j in range(ST):
                        tt = nc.tensor.transpose(bank[j // 4][:, j % 4 * P:(j % 4 + 1) * P], xg[:, en.b, j, 0:D],
                                                 ident[:, :])
                        if j == 3 or j == ST - 1:
                            tt.then_inc(S.xgT_done, 1)

            lagged_steps(pe, expert_step, NE, True)

        @block.vector
        def _(dve):
            v = nc.vector
            dve.wait_ge(S.const_loaded, 16)
            casts = [
                v.tensor_copy(ident_b[:, :], ident),
                v.tensor_copy(before_b[:, :], field("before")),
                v.memset(ones_b[:, :], 1.0),
                v.tensor_copy(maskq_b[:, :], field("maskq")),
                v.tensor_copy(comb_st[0:WIN], field("comb")[0:WIN].unsqueeze(1).broadcast_to([WIN, H, P])),
                v.tensor_copy(comb_st[WIN:WIN + 3 * H],
                              field("head_rows")[WIN:WIN + 3 * H].unsqueeze(2).broadcast_to([3 * H, H, P])),
                v.tensor_copy(comb_mv[0:WIN], field("eye2")[0:WIN].unsqueeze(1).broadcast_to([WIN, 2, P])),
                v.memset(qk[:, :, :, :, :], 0.0),
                v.memset(v_cur[:, :, :, DH:DH + 1], 1.0),
                v.memset(v_mix[:, :, :, DH:DH + 1], 1.0),
                v.memset(v_mix[0:WIN, 0, :, 0:DH], 0.0),
                v.memset(macc[:, 0], 0.0),
                v.tensor_copy(kT[:, 0, :, 0:WIN],
                              pen[:, T // P - 1:T // P].unsqueeze(2).broadcast_to([P, NG, WIN])),
                v.memset(es[:, :], 0.0),
            ]
            for ins in casts:
                ins.then_inc(S.casts, 1)
            dve.wait_ge(S.casts, 8)
            v.memset(qk[:, :, 0, :, PEN_ROW:PEN_ROW + 1], 1.0).then_inc(S.casts, 1)
            v.memset(geq[:, :, :], 0.0).then_inc(S.casts, 1)
            dve.wait_ge(S.cent_len, 3)
            v.tensor_scalar(cent_sq[:, :], cent[:, :], cent_n[:, 2:3], None, ALU.mult).then_inc(S.cent_unit, 1)
            dve.wait_ge(S.centT_done, 1)
            v.tensor_copy(centT[:, :], bank[0][:, 0:NGR + NE]).then_inc(S.centT_evac, 1)
            dve.wait_ge(S.x_loaded, 16)
            dve.wait_ge(S.w_loaded, 16 * 21)

            def step(tau, tn, tf, tp, tw, tr):
                if tp is not None:
                    m = mx[:, tp.b].rearrange("p (g s) -> p g s", g=NG)
                    for u in range(8):
                        s, g2 = u % NS, u // NS
                        dve.wait_ge(S.p1_scores, 8 * tp.n + (u + 1))
                        v.tensor_reduce(m[:, 2 * g2:2 * g2 + 2, s],
                                        bank[u % 2][:, 0:2 * SPAN].rearrange("p (c j) -> p c j", c=2),
                                        AX.X, ALU.max).then_inc(S.p1_reduced, 1)
                    dve.wait_ge(S.p1_reduced, 8 * tp.n + 8)
                    v.tensor_scalar(mp[:, tp.b, 0], mx[:, tp.b], -1.0, None, ALU.mult).then_inc(S.negm, 1)
                    dve.wait_ge(S.negm, 4 * tp.n + 1)
                    v.scalar_tensor_tensor(nm[:, :], mx[:, tp.b], -1.0, mp[:, tp.b, 0], ALU.mult,
                                           ALU.subtract).then_inc(S.negm, 1)
                    dve.wait_ge(S.negm, 4 * tp.n + 2)
                    v.tensor_copy(mp[:, tp.b, 1], nm[:, :]).then_inc(S.negm, 1)
                    dve.wait_ge(S.negm, 4 * tp.n + 3)
                    v.tensor_tensor(mp[:, tp.b, 2], nm[:, :], mp[:, tp.b, 1], ALU.subtract).then_inc(S.negm, 1)
                if tw is not None:
                    dve.wait_ge(S.wout_done, tw.n + 1)
                    xt = x_all[:, bass.ds(tw.n, 1), :].rearrange("p o d -> p (o d)")
                    v.tensor_tensor(xt, xt, bank[7][:, 3 * P:4 * P], ALU.add).then_inc(S.x1_ready, 1)
                if tr is not None:
                    dve.wait_ge(S.router_done, tr.n + 1)
                    v.tensor_scalar(sc[:, :], bank[3][:, 0:NGR + NE], pout[:, 1 - tr.b, 2:3], None, ALU.mult)\
                     .then_inc(S.sc_ready, 1)
                if tp is not None:
                    dve.wait_ge(S.mT_done, tp.n + 1)
                    wait(dve, S.p2_scores, NS * (tp.n - 1))
                    v.tensor_copy(comb_mv[WIN:WIN + 3 * H, tp.b, :], bank[6][:, :].bitcast(BF16)[0:3 * H, 0:P])\
                     .then_inc(S.mT_evac, 1)
                if tf is not None:
                    dve.wait_ge(S.qkv_done, tf.n + 1)
                    wait(dve, S.rope_r, tf.n)
                    z = bank[4][:, 0:2 * D].rearrange("p (h c i) -> p h c i", c=2, i=HALF)
                    zb = rb[:, :].rearrange("p (h c i) -> p h c i", c=2, i=HALF)
                    ct = cos[:, bass.ds(tf.n, 1), :].broadcast_to([P, 4 * H, HALF])
                    stn = sin[:, bass.ds(tf.n, 1), :].broadcast_to([P, 2 * H, HALF])
                    v.tensor_tensor(ra[:, :].rearrange("p (m i) -> p m i", i=HALF),
                                    bank[4][:, 0:2 * D].rearrange("p (m i) -> p m i", i=HALF), ct,
                                    ALU.mult).then_inc(S.rope_ab, 1)
                    v.scalar_tensor_tensor(zb[:, :, 0], z[:, :, 1], -1.0, stn, ALU.mult, ALU.mult)\
                     .then_inc(S.rope_ab, 1)
                    v.tensor_tensor(zb[:, :, 1], z[:, :, 0], stn, ALU.mult).then_inc(S.rope_ab, 1)
                if tw is not None:
                    dve.wait_ge(S.x1_ready, tw.n + 1)
                    hold(dve)
                    v.bn_stats(st2[:, :], x_all[:, bass.ds(tw.n, 1), :].rearrange("p o d -> p (o d)"))\
                     .then_inc(S.ln2, 1)
                    dve.wait_ge(S.ln2, 6 * tw.n + 1)
                    hold(dve)
                    v.bn_aggr(mv2[:, tw.b], st2[:, :]).then_inc(S.ln2, 1)
                    c = 1 - tw.b
                    dve.wait_ge(S.ln2, 6 * tw.n + 2)
                    v.tensor_scalar(pin[:, c, 1:2], mv2[:, tw.b, 1:2], EPS, None, ALU.add).then_inc(S.ln2, 1)
                    dve.wait_ge(S.ln2, 6 * tw.n + 3)
                    v.reciprocal(ve[:, 0:1], pin[:, c, 1:2]).then_inc(S.ln2, 1)
                    dve.wait_ge(S.ln2, 6 * tw.n + 4)
                    v.tensor_scalar(ve[:, 1:2], ve[:, 0:1], mv2[:, tw.b, 1:2], float(D), ALU.mult, ALU.mult)\
                     .then_inc(S.ln2, 1)
                    dve.wait_ge(S.ln2, 6 * tw.n + 5)
                    v.tensor_scalar(pin[:, c, 2:3], ve[:, 1:2], 1e-24, None, ALU.max).then_inc(S.ln2, 1)
                if tn is not None:
                    v.bn_stats(st1[:, :], x_all[:, bass.ds(tn.n, 1), :].rearrange("p o d -> p (o d)"))\
                     .then_inc(S.ln1, 1)
                    dve.wait_ge(S.ln1, 3 * tn.n + 1)
                    hold(dve)
                    v.bn_aggr(mv1[:, tn.b], st1[:, :]).then_inc(S.ln1, 1)
                    dve.wait_ge(S.ln1, 3 * tn.n + 2)
                    v.tensor_scalar(pin[:, tn.b, 0:1], mv1[:, tn.b, 1:2], EPS, None, ALU.add).then_inc(S.ln1, 1)
                if tr is not None:
                    n = tr.n
                    R = 12
                    dve.wait_ge(S.sc_ready, n + 1)
                    v.tensor_tensor(es[:, :], sc[:, NGR:NGR + NE], bias_b[:, :], ALU.add).then_inc(S.route, 1)
                    v.max(gm8[:, :], sc[:, 0:NGR]).then_inc(S.route, 1)
                    dve.wait_ge(S.route, R * n + 2)
                    hold(dve)
                    v.max_index(gi8[:, :], gm8[:, :], sc[:, 0:NGR]).then_inc(S.route, 1)
                    dve.wait_ge(S.route, R * n + 3)
                    v.tensor_tensor(geq[:, :, :], numbers[:, 0:NGR].unsqueeze(2).broadcast_to([P, NGR, TOPG]),
                                    gi8[:, 0:TOPG].unsqueeze(1).broadcast_to([P, NGR, TOPG]), ALU.is_equal)\
                     .then_inc(S.route, 1)
                    dve.wait_ge(S.route, R * n + 4)
                    v.tensor_reduce(gsel[:, :], geq[:, :, :], AX.X, ALU.add).then_inc(S.route, 1)
                    dve.wait_ge(S.route, R * n + 5)
                    v.tensor_scalar(gpen[:, :], gsel[:, :], 1e9, -1e9, ALU.mult, ALU.add).then_inc(S.route, 1)
                    by_group = lambda ap: ap.rearrange("p (g e) -> p g e", g=NGR)
                    v.tensor_tensor(by_group(es2[:, :]), by_group(es[:, :]),
                                    gsel[:, :].unsqueeze(2).broadcast_to([P, NGR, EPG]), ALU.mult)\
                     .then_inc(S.route, 1)
                    dve.wait_ge(S.route, R * n + 7)
                    v.tensor_tensor(by_group(es[:, :]), by_group(es2[:, :]),
                                    gpen[:, :].unsqueeze(2).broadcast_to([P, NGR, EPG]), ALU.add)\
                     .then_inc(S.route, 1)
                    dve.wait_ge(S.route, R * n + 8)
                    hold(dve)
                    v.max(em8[:, :], es[:, :]).then_inc(S.route, 1)
                    dve.wait_ge(S.route, R * n + 9)
                    hold(dve)
                    wait(dve, S.gate_exp, n - 1)
                    v.tensor_scalar(ed4[:, tr.b], em8[:, 0:TOPK], em8[:, 0:1], None, ALU.subtract)\
                     .then_inc(S.route, 1)
                    v.max_index(ei8[:, :], em8[:, :], es[:, :]).then_inc(S.route, 1)
                    dve.wait_ge(S.route, R * n + 11)
                    v.tensor_tensor(oh[:, :, :], numbers.unsqueeze(1).broadcast_to([P, TOPK, NE]),
                                    ei8[:, 0:TOPK].unsqueeze(2).broadcast_to([P, TOPK, NE]), ALU.is_equal)\
                     .then_inc(S.route, 1)
                    dve.wait_ge(S.route, R * n + 12)
                    wait(dve, S.pos_done, n - 1)
                    with nc.allow_low_precision("marks are 0 or 1"):
                        v.tensor_reduce(msel[:, tr.b], oh[:, :, :].rearrange("p k e -> p e k"), AX.X, ALU.add)\
                         .then_inc(S.sel_ready, 1)
                if tn is not None:
                    dve.wait_ge(S.pow_done, tau + 2)
                    wait(dve, S.xnT_done, tn.n - 1)
                    v.tensor_scalar(xn[:, tn.b], x_all[:, bass.ds(tn.n, 1), :].rearrange("p o d -> p (o d)"),
                                    mv1[:, tn.b, 0:1], pout[:, tn.b, 0:1], ALU.subtract, ALU.mult)\
                     .then_inc(S.xn_ready, 1)
                if tw is not None:
                    dve.wait_ge(S.pow_done, tau + 2)
                    wait(dve, dispatched[tw.b], 16 * TOPK * tw.half)
                    wait(dve, S.xfT_done, tw.n - 1)
                    v.tensor_scalar(xfe[:, tw.b, :, 0:D], x_all[:, bass.ds(tw.n, 1), :].broadcast_to([P, TOPK, D]),
                                    mv2[:, tw.b, 0:1], pout[:, 1 - tw.b, 1:2], ALU.subtract, ALU.mult)\
                     .then_inc(S.xf_ready, 1)
                if tf is not None:
                    dve.wait_ge(S.kT_evac, tf.n + 1)
                    wait(dve, S.p2_scores, NS * tf.n)
                    v.tensor_scalar(kT[:, 1 - tf.b, :, 0:WIN], kT[:, tf.b, :, P:SPAN].bitcast(F32),
                                    pen[:, bass.ds(tf.n, 1)], None, ALU.add).then_inc(S.k_prev, 1)
                if tp is not None:
                    dve.wait_ge(S.pv_done, tp.n + 1)
                    wait(dve, S.oT_done, tp.n - 1)
                    pv = bank[7][:, 0:2 * H * (DH + 1)].rearrange("p (m c d) -> p m c d", c=2, d=DH + 1)
                    for par in range(2):
                        rows = slice(WIN * par, WIN * (par + 1))
                        v.reciprocal(rec[rows, tp.b], pv[rows, :, par, DH]).then_inc(S.recip, 1)
                    for par in range(2):
                        rows = slice(WIN * par, WIN * (par + 1))
                        dve.wait_ge(S.recip, 2 * tp.n + (par + 1))
                        v.tensor_tensor(on[rows, tp.b].rearrange("p b (m d) -> p (b m) d", d=DH),
                                        pv[rows, :, par, 0:DH],
                                        rec[rows, tp.b].unsqueeze(2).broadcast_to([WIN, H, DH]), ALU.mult)\
                         .then_inc(S.onorm, 1)
                if tr is not None:
                    n = tr.n
                    dve.wait_ge(S.pos_done, n + 1)
                    v.tensor_tensor(macc[:, 1 - tr.b], macc[:, tr.b], msel[:, tr.b], ALU.add).then_inc(S.acc_ready, 1)
                    v.tensor_tensor(ohp[:, :, :], oh[:, :, :],
                                    bank[3][:, P:P + NE].unsqueeze(1).broadcast_to([P, TOPK, NE]), ALU.mult)\
                     .then_inc(S.pos_read, 1)
                    dve.wait_ge(S.pos_read, n + 1)
                    v.tensor_reduce(posk[:, :], ohp[:, :, :], AX.X, ALU.add).then_inc(S.slots, 1)
                    dve.wait_ge(S.slots, 4 * n + 1)
                    v.tensor_scalar(keep[:, :], posk[:, :], float(cap), None, ALU.is_lt).then_inc(S.slots, 1)
                    v.scalar_tensor_tensor(slotf[:, :], ei8[:, 0:TOPK], float(cap), posk[:, :], ALU.mult,
                                           ALU.add).then_inc(S.slots, 1)
                    dve.wait_ge(S.slots, 4 * n + 3)
                    v.scalar_tensor_tensor(slotf2[:, :], keep[:, :], -OOB, slotf[:, :], ALU.mult, ALU.add)\
                     .then_inc(S.slots, 1)
                    dve.wait_ge(S.slots, 4 * n + 4)
                    wait(dve, dispatched[tr.b], 16 * TOPK * tr.half)
                    v.tensor_scalar(sidx[:, tr.b], slotf2[:, :], OOB, None, ALU.add).then_inc(S.slot_ready, 1)
                    dve.wait_ge(S.gate_exp, n + 1)
                    v.reciprocal(exr[:, :], exs[:, tr.b]).then_inc(S.gate_done, 1)
                    dve.wait_ge(S.gate_done, 2 * n + 1)
                    v.scalar_tensor_tensor(gates[:, bass.ds(n, 1), :].rearrange("p o k -> p (o k)"), ex4[:, tr.b],
                                           exr[:, :], keep[:, :], ALU.mult, ALU.mult).then_inc(S.gate_done, 1)

            attention_steps(dve, step)

            def shared_step(m, md):
                if m is not None:
                    for h in range(2):
                        dve.wait_ge(S.sh_act, 2 * m.n + (h + 1))
                        dve.wait_ge(S.sh_gu, 4 * m.n + (2 * h + 2))
                        v.tensor_tensor(sact[:, m.b, h], sact[:, m.b, h], bank[2 + h][:, :], ALU.mult)\
                         .then_inc(S.sh_mul, 1)
                if md is not None:
                    dve.wait_ge(S.sh_down, md.n + 1)
                    xs = x_all[:, bass.ds(4 * md.n, 4), :]
                    v.tensor_tensor(xs, xs, bank[4 + md.b][:, :].rearrange("p (t d) -> p t d", d=D), ALU.add)\
                     .then_inc(S.sh_added, 1)

            lagged_steps(dve, shared_step, N // 512, False)

            def expert_step(en, e, ed):
                def times_up(ch):
                    for h in range(2):
                        dve.wait_ge(S.h_act, 4 * e.n + (2 * ch + h + 1))
                        dve.wait_ge(S.gu_done, 8 * e.n + (4 * ch + 2 * h + 2))
                        hs = hact[:, e.b, h, ch * CH:(ch + 1) * CH]
                        v.tensor_tensor(hs, hs, bank[4 + h][:, 0:CH], ALU.mult).then_inc(S.h_mul, 1)

                if e is not None:
                    times_up(0)
                    times_up(1)
                if en is not None:
                    dve.wait_ge(xg_arrived[en.b], 16 * (en.half + 1))
                    wait(dve, y_sent[en.b], 16 * ST * en.half)
                    v.tensor_copy(yidx[:, en.b], xg[:, en.b, :, D]).then_inc(S.yidx_ready, 1)
                    wait(dve, S.gu_done, 8 * (en.n - 1))
                    dve.wait_ge(S.xgT_done, 2 * en.n + 1)
                    v.tensor_copy(xgT[:, en.b, 0:4 * P], bank[0][:, :]).then_inc(S.xgT_evac, 1)
                    dve.wait_ge(S.xgT_done, 2 * en.n + 2)
                    v.tensor_copy(xgT[:, en.b, 4 * P:cap], bank[1][:, 0:cap - 4 * P]).then_inc(S.xgT_evac, 1)

            lagged_steps(dve, expert_step, NE, True)

            dve.wait_ge(S.sh_added, N // 512)
            with dve.Fori(0, NT // 4) as i:
                for c in range(4):
                    t = 4 * i + c
                    xt = x_all[:, bass.ds(t, 1), :].rearrange("p o d -> p (o d)")
                    dve.wait_ge(r_arrived[c], 16 * (i + 1))
                    for k in range(TOPK):
                        if k:
                            dve.wait_ge(S.comb_step, TOPK * t + k)
                        gk = gates[:, bass.ds(t, 1), k:k + 1].rearrange("p o k -> p (o k)")
                        v.scalar_tensor_tensor(xt, rload[:, c, k], gk, xt, ALU.mult, ALU.add)\
                         .then_inc(S.comb_step, 1)


_INS = ["L0_attn_x", "L0_attn_Wqkv", "L0_attn_Wout", "L0_ffn_group_centroids", "L0_ffn_expert_centroids",
        "L0_ffn_bias", "L0_ffn_wg", "L0_ffn_wu", "L0_ffn_wd", "L0_ffn_sg", "L0_ffn_su", "L0_ffn_sd"]


def kernel(**inputs):
    import numpy as _np
    import concourse.bacc as _bacc
    from concourse import mybir as _mybir
    from concourse.bass_utils import run_bass_kernel_spmd as _run

    nc = _bacc.Bacc("TRN2", target_bir_lowering=False, num_devices=1)
    arrays, args = {}, []
    for name in _INS:
        a = _np.ascontiguousarray(inputs[name])
        arrays[f"in_{name}_dram"] = a
        args.append(nc.dram_tensor(f"in_{name}_dram", a.shape, _mybir.dt.from_np(a.dtype), kind="ExternalInput").ap())
    shape = inputs["L0_attn_x"].shape
    const, where, cap = constants(shape[0] * shape[1], shape[1])
    arrays["constants_dram"] = const
    args.append(nc.dram_tensor("constants_dram", const.shape, _mybir.dt.float32, kind="ExternalInput").ap())
    args.append(nc.dram_tensor("out_0_dram", shape, _mybir.dt.float32, kind="ExternalOutput").ap())
    block_kernel(nc, *args, where, cap)
    r = _run(nc, [arrays], core_ids=[0])
    return r.results[0]["out_0_dram"]
```

```python
from collections import namedtuple
from contextlib import ExitStack

import concourse.bass as bass
from concourse import mybir

F32 = mybir.dt.float32
F32R = mybir.dt.float32r
BF16 = mybir.dt.bfloat16
U32 = mybir.dt.uint32
ALU = mybir.AluOpType
ACT = mybir.ActivationFunctionType
AX = mybir.AxisListType

P = 128
H, DH, WIN = 16, 8, 64
HALF = DH // 2
STRIP = 64
NS = P // STRIP
NG = H // NS
Q_HI, Q_MID, Q_LO = slice(0, 7, 3), slice(1, 5, 3), slice(2, 3)
K_HI, K_MID, K_LO = slice(0, 3), slice(3, 5), slice(6, 7)
PEN_ROW = 7 * DH
NU = H // 4
NEG = -1e30
NE, NGR, TOPG, TOPK = 32, 8, 4, 4
EPG = NE // NGR
FF = 256
EPS = 1e-5

Tile = namedtuple("Tile", "n half b")


def tile_of(half, b):
    return Tile(2 * half + b, half, b)


def constants(N, T):
    import numpy as np

    cap = max(1, int(N / NE * TOPK * 1.25))
    p = np.arange(P)
    theta = (1.0 / np.float32(10000.0) ** (np.arange(HALF, dtype=np.float32) / np.float32(HALF))).astype(np.float32)
    pos = (np.arange(N) % T).astype(np.float32)
    freq = (pos[:, None] * theta[None, :]).astype(np.float32)
    per_tile = lambda a: a.reshape(N // P, P, HALF).transpose(1, 0, 2).reshape(P, -1)
    pen = np.zeros((P, N // P), np.float32)
    pen[PEN_ROW::STRIP, ::T // P] = NEG
    kb = np.arange(P)[None, :]
    qb = np.arange(WIN)[:, None]
    comb = np.zeros((P, P), np.float32)
    comb[:WIN] = np.where((kb > qb) & (kb <= qb + WIN), 0.0, NEG)
    head_rows = np.zeros((P, H), np.float32)
    for part in range(3):
        head_rows[WIN + part * H:WIN + (part + 1) * H] = np.eye(H)
    fields = {
        "cos": per_tile(np.cos(freq)),
        "sin": per_tile(np.sin(freq)),
        "pen": pen,
        "ident": np.eye(P),
        "before": (p[:, None] < p[None, :]),
        "maskq": np.where((kb > p[:, None] % WIN) & (kb <= p[:, None] % WIN + WIN), 0.0, NEG),
        "comb": comb,
        "head_rows": head_rows,
        "eye2": np.concatenate([np.eye(P)[:, :WIN], np.eye(P)[:, :WIN]], 1),
        "numbers": np.tile(np.arange(NE), (P, 1)),
        "pair": ((np.arange(N // P)[None, :, None] * P + p[:, None, None]) * TOPK + np.arange(TOPK)).reshape(P, -1),
    }
    at, where = 0, {}
    for name, a in fields.items():
        where[name] = (at, a.shape[1])
        at += a.shape[1]
    return np.concatenate([np.asarray(a, np.float32) for a in fields.values()], 1), where, cap


def block_kernel(nc, x, w_qkv, w_out, group_c, expert_c, bias, w_g, w_u, w_d, s_g, s_u, s_d, const, out, where, cap):
    BT, T, D = x.shape
    N = BT * T
    NT = N // P
    NSLOT = NE * cap
    ST = cap // P
    SPAN = P + WIN
    ROW = D + 1
    OOB = float(1 << 20)
    QK_SCALE = float(DH) ** -0.5
    CH = cap // 2
    assert D == P and cap % P == 0 and NT % 2 == 0 and H * DH == D

    x_v = x.rearrange("b (t p) d -> p (b t) d", p=P)
    out_v = out.rearrange("b (t p) d -> p (b t) d", p=P)
    slots_d = nc.dram_tensor("expert_slots", [NSLOT, ROW], F32, kind="Internal").ap()
    pairs_d = nc.dram_tensor("pair_results", [N * TOPK, D], F32, kind="Internal").ap()
    slots_v = slots_d.rearrange("(e p j) c -> e p (j c)", p=P, j=ST)
    pairs_v = pairs_d.rearrange("(t p k) d -> t p (k d)", p=P, k=TOPK)

    with ExitStack() as ctx:
        def sb(name, shape, dt=F32):
            return ctx.enter_context(nc.sbuf_tensor(name, shape, dt))

        def sem(name):
            return ctx.enter_context(nc.semaphore(name))

        bank = [ctx.enter_context(nc.psum_tensor(f"bank{i}", [P, 512], F32)) for i in range(8)]

        x_all = sb("x_all", [P, NT, D])
        xfT_all = sb("xfT_all", [P, N])
        gates = sb("gates", [P, NT, TOPK])
        cst = sb("cst", [P, const.shape[1]])

        def field(name):
            at, n = where[name]
            return cst[:, at:at + n]

        cos = field("cos").rearrange("p (t i) -> p t i", i=HALF)
        sin = field("sin").rearrange("p (t i) -> p t i", i=HALF)
        pen = field("pen")
        ident = field("ident")
        numbers = field("numbers")
        pair = field("pair").rearrange("p (t k) -> p t k", k=TOPK)

        wqkv = sb("wqkv", [P, 3 * D])
        wout = sb("wout", [P, D])
        ident_b = sb("ident_b", [P, P], BF16)
        before_b = sb("before_b", [P, P], BF16)
        ones_b = sb("ones_b", [P, P], BF16)
        maskq_b = sb("maskq_b", [P, P], BF16)
        comb_st = sb("comb_st", [P, H, P], BF16)
        comb_mv = sb("comb_mv", [P, 2, P], BF16)
        cent = sb("cent", [NGR + NE, D])
        cent_sq = sb("cent_sq", [NGR + NE, D])
        cent_n = sb("cent_n", [NGR + NE, 4])
        centT = sb("centT", [P, NGR + NE])
        bias_b = sb("bias_b", [P, NE])
        mhalf = sb("mhalf", [P, 4])
        st1 = sb("st1", [P, 6])
        st2 = sb("st2", [P, 6])
        mv1 = sb("mv1", [P, 2, 2])
        mv2 = sb("mv2", [P, 2, 2])
        pin = sb("pin", [P, 2, 3])
        pout = sb("pout", [P, 2, 3])
        ve = sb("ve", [P, 2])
        xn = sb("xn", [P, 2, D])
        xnT = sb("xnT", [P, 2, P])
        ra = sb("ra", [P, 2 * D])
        rb = sb("rb", [P, 2 * D])
        rr = sb("rr", [P, 2, 2 * D])
        r1 = sb("r1", [P, 2 * D])
        qk = sb("qk", [P, 2, 2, H, 8, DH], BF16)
        qT = sb("qT", [P, 2, NG, P], BF16)
        kT = sb("kT", [P, 2, NG, SPAN], BF16)
        v_cur = sb("v_cur", [P, 2, H, 32])
        v_mix = sb("v_mix", [P, 2, H, 32])
        mx = sb("mx", [P, 2, H])
        nm = sb("nm", [P, H])
        mp = sb("mp", [P, 2, 3, H], BF16)
        pt = sb("pt", [P, 2, NU, 512])
        pvT = sb("pvT", [P, 2, 512])
        rec = sb("rec", [P, H])
        on = sb("on", [P, 2, D])
        oT = sb("oT", [P, 2, P])
        xfe = sb("xfe", [P, 2, TOPK, ROW])
        xfT = sb("xfT", [P, 2, P])
        sc = sb("sc", [P, NGR + NE])
        es = sb("es", [P, NE])
        es2 = sb("es2", [P, NE])
        gm8 = sb("gm8", [P, 8])
        gi8 = sb("gi8", [P, 8], U32)
        geq = sb("geq", [P, NGR, TOPG])
        gsel = sb("gsel", [P, NGR])
        gpen = sb("gpen", [P, NGR])
        em8 = sb("em8", [P, 8])
        ei8 = sb("ei8", [P, 8], U32)
        ed4 = sb("ed4", [P, 2, TOPK])
        ex4 = sb("ex4", [P, 2, TOPK])
        exs = sb("exs", [P, 2, 1])
        exr = sb("exr", [P, 1])
        oh = sb("oh", [P, TOPK, NE])
        msel = sb("msel", [P, 2, NE], BF16)
        macc = sb("macc", [P, 2, NE], BF16)
        ohp = sb("ohp", [P, TOPK, NE])
        posk = sb("posk", [P, TOPK])
        keep = sb("keep", [P, TOPK])
        slotf = sb("slotf", [P, TOPK])
        slotf2 = sb("slotf2", [P, TOPK])
        sidx = sb("sidx", [P, 2, TOPK], U32)
        sgw = sb("sgw", [P, FF])
        suw = sb("suw", [P, FF])
        sdw = sb("sdw", [P, 2, D])
        wgu = sb("wgu", [P, 2, 2, FF])
        wdn = sb("wdn", [P, 2, 2, D])
        sact = sb("sact", [P, 2, 2, 512])
        fill = sb("fill", [P, ST, ROW])
        xg = sb("xg", [P, 2, ST, ROW])
        xgT = sb("xgT", [P, 2, cap])
        hact = sb("hact", [P, 2, 2, cap])
        yout = sb("yout", [P, 2, ST, D])
        ypair = sb("ypair", [P, 2, ST])
        yidx = sb("yidx", [P, 2, ST], U32)
        rload = sb("rload", [P, 4, TOPK, D])

        names = """const_loaded x_loaded w_loaded cent_loaded fill_done zero_done filled zeroed
        cent_sum cent_len cent_unit centT_done centT_evac casts
        ln1 ln2 pow_done xn_ready xnT_done xnT_evac qkv_done rope_ab rope_r v_evac
        v_prev split_hi split_rest split_mid split_lo qkT_done qT_evac kT_evac k_prev p1_scores p1_reduced negm mT_done mT_evac
        p2_scores exp_done pv_done pv_evac pvT_done recip onorm oT_done oT_evac wout_done x1_ready xf_ready xfe_id
        xfT_done xfT_evac xfT_kept router_done sc_ready route gate_exp gate_done sel_ready acc_ready pos_done
        pos_read slots slot_ready sh_gu sh_act sh_mul sh_down sh_added
        xgT_done xgT_evac gu_done h_act h_mul down_done y_evac ypair_ready yidx_ready comb_step stored""".split()
        S = namedtuple("Semaphores", names)(*[sem(n) for n in names])
        dispatched = [sem(f"dispatched{b}") for b in range(2)]
        wgu_arrived = [sem(f"wgu_arrived{b}") for b in range(2)]
        wdn_arrived = [sem(f"wdn_arrived{b}") for b in range(2)]
        xg_arrived = [sem(f"xg_arrived{b}") for b in range(2)]
        y_sent = [sem(f"y_sent{b}") for b in range(2)]
        r_arrived = [sem(f"r_arrived{b}") for b in range(4)]

        def wait(eng, s, value):
            if not (isinstance(value, int) and value < 1):
                eng.wait_ge(s, value)

        def hold(eng):
            eng.nop(nofuse=True)

        def attention_steps(eng, step):
            FIRST = 6
            LAST = FIRST + (NT - 1 - FIRST) // 2 * 2

            def straight(tau):
                step(tau, *[tile_of((tau - k) // 2, (tau - k) % 2) if 0 <= tau - k < NT else None
                            for k in range(-1, 5)])

            for tau in range(-1, FIRST):
                straight(tau)
            with eng.Fori(0, (LAST - FIRST) // 2) as i:
                for c in range(2):
                    step(2 * i + (FIRST + c), *[tile_of(i + (FIRST + c - k) // 2, (FIRST + c - k) % 2)
                                                for k in range(-1, 5)])
            for tau in range(LAST, NT + 4):
                straight(tau)

        def lagged_steps(eng, step, count, ahead):
            FIRST = 3
            LAST = FIRST + (count - 1 - FIRST) // 2 * 2
            lags = range(-1 if ahead else 0, 2)

            def straight(n):
                step(*[tile_of((n - k) // 2, (n - k) % 2) if 0 <= n - k < count else None for k in lags])

            for n in range(-1 if ahead else 0, FIRST):
                straight(n)
            with eng.Fori(0, (LAST - FIRST) // 2) as i:
                for c in range(2):
                    step(*[tile_of(i + (FIRST + c - k) // 2, (FIRST + c - k) % 2) for k in lags])
            for n in range(LAST, count + 1):
                straight(n)

        block = ctx.enter_context(nc.Block())

        @block.sync
        def _(sp):
            sp.dma_start(cst[:, :], const).then_inc(S.const_loaded, 16)
            sp.dma_start(x_all[:, :, :], x_v).then_inc(S.x_loaded, 16)

            def load_wgu(e, c):
                sp.dma_start(wgu[:, c, 0], w_g[e]).then_inc(wgu_arrived[c], 16)
                sp.dma_start(wgu[:, c, 1], w_u[e]).then_inc(wgu_arrived[c], 16)

            def load_wdn(e, c):
                sp.dma_start(wdn[:, c], w_d[e].rearrange("(h p) n -> p h n", p=P)).then_inc(wdn_arrived[c], 16)

            def load_slots(e, c):
                sp.dma_start(xg[:, c].rearrange("p j c -> p (j c)"), slots_v[e]).then_inc(xg_arrived[c], 16)

            for e in range(2):
                load_wgu(e, e)
                load_wdn(e, e)
            sp.wait_ge(S.fill_done, 2)
            with sp.Fori(0, NE) as e:
                sp.dma_start(slots_v[e], fill[:, :, :].rearrange("p j c -> p (j c)")).then_inc(S.filled, 16)
            sp.wait_ge(S.zero_done, 1)
            with sp.Fori(0, NT) as t:
                sp.dma_start(pairs_v[t], rload[:, 0].rearrange("p k d -> p (k d)")).then_inc(S.zeroed, 16)

            for b in range(2):
                sp.wait_ge(dispatched[b], 16 * TOPK * (NT // 2))
            for e in range(2):
                load_slots(e, e)
            with sp.Fori(0, (NE - 2) // 2) as i:
                for c in range(2):
                    e = 2 * i + (2 + c)
                    sp.wait_ge(S.xgT_done, 2 * (e - 1))
                    sp.wait_ge(S.ypair_ready, e - 1)
                    load_slots(e, c)
                    sp.wait_ge(S.gu_done, 8 * (e - 1))
                    load_wgu(e, c)
                    sp.wait_ge(S.down_done, e - 1)
                    load_wdn(e, c)

            for b in range(2):
                sp.wait_ge(y_sent[b], 16 * ST * (NE // 2))
            sp.wait_ge(S.zeroed, 16 * NT)
            for c in range(4):
                sp.dma_start(rload[:, c].rearrange("p k d -> p (k d)"), pairs_v[c]).then_inc(r_arrived[c], 16)
            with sp.Fori(0, NT // 4 - 1) as i:
                for c in range(4):
                    sp.wait_ge(S.comb_step, TOPK * (4 * i + (c + 1)))
                    sp.dma_start(rload[:, c].rearrange("p k d -> p (k d)"), pairs_v[4 * i + (c + 4)])\
                      .then_inc(r_arrived[c], 16)

        @block.gpsimd
        def _(pool):
            g = nc.gpsimd
            g.memset(mhalf[:, :], -0.5).then_inc(S.cent_len, 1)
            g.memset(fill[:, :, 0:D], 0.0).then_inc(S.fill_done, 1)
            g.memset(fill[:, :, D:ROW], OOB).then_inc(S.fill_done, 1)
            g.memset(rload[:, 0], 0.0).then_inc(S.zero_done, 1)
            pool.wait_ge(S.cent_sum, 1)
            pool.wait_ge(S.cent_len, 1)
            g.tensor_scalar(cent_n[:, 1:2], cent_n[:, 0:1], 1e-24, None, ALU.max).then_inc(S.cent_len, 1)
            pool.wait_ge(S.cent_len, 2)
            g.tensor_tensor(cent_n[:, 2:3], cent_n[:, 1:2], mhalf[0:NGR + NE, 0:1], ALU.pow).then_inc(S.cent_len, 1)

            def step(tau, tn, tf, tp, ts, tw, tr):
                if tf is not None:
                    b = tf.b
                    pool.wait_ge(S.rope_ab, 3 * tf.n + 3)
                    wait(pool, S.split_hi, 2 * (tf.n - 1))
                    wait(pool, S.split_rest, tf.n - 1)
                    g.tensor_tensor(rr[:, b], ra[:, :], rb[:, :], ALU.add).then_inc(S.rope_r, 1)
                if tr is not None:
                    pool.wait_ge(S.xfT_evac, tr.n + 1)
                    hold(pool)
                    g.tensor_copy(xfT_all[:, bass.ts(tr.n, P)], xfT[:, tr.b]).then_inc(S.xfT_kept, 1)
                if tf is not None:
                    pool.wait_ge(S.split_mid, 2 * tf.n + 2)
                    r = r1[:, :].rearrange("p (w h d) -> p w h d", w=2, h=H)
                    g.tensor_tensor(qk[:, b, 0, :, 2, :], r[:, 0], qk[:, b, 0, :, 4, :], ALU.subtract)\
                     .then_inc(S.split_lo, 1)
                    g.tensor_tensor(qk[:, b, 1, :, 6, :], r[:, 1], qk[:, b, 1, :, 4, :], ALU.subtract)\
                     .then_inc(S.split_lo, 1)
                if tw is not None or tn is not None:
                    lo, hi = (0 if tn is not None else 1), (3 if tw is not None else 1)
                    c = tn.b if tn is not None else tw.b
                    if tn is not None:
                        pool.wait_ge(S.ln1, 3 * tn.n + 3)
                    if tw is not None:
                        pool.wait_ge(S.ln2, 6 * tw.n + 6)
                    if isinstance(tau, int) and tau == -1:
                        pool.wait_ge(S.cent_len, 1)
                    g.tensor_tensor(pout[:, c, lo:hi], pin[:, c, lo:hi], mhalf[:, lo:hi], ALU.pow)\
                     .then_inc(S.pow_done, 1)
                if tw is not None:
                    wait(pool, dispatched[tw.b], 16 * TOPK * tw.half)
                    hold(pool)
                    g.tensor_copy(xfe[:, tw.b, :, D:ROW], pair[:, bass.ds(tw.n, 1), :].rearrange("p o k -> p k o"))\
                     .then_inc(S.xfe_id, 1)
                if tr is not None:
                    if isinstance(tr.n, int) and tr.n == 0:
                        pool.wait_ge(S.filled, 16 * NE)
                    pool.wait_ge(S.slot_ready, tr.n + 1)
                    pool.wait_ge(S.xfe_id, tr.n + 1)
                    pool.wait_ge(S.xf_ready, tr.n + 1)
                    hold(pool)
                    for k in range(TOPK):
                        g.indirect_dma_start(
                            out=slots_d, out_offset=bass.IndirectOffsetOnAxis(ap=sidx[:, tr.b, k:k + 1], axis=0),
                            in_=xfe[:, tr.b, k, :], in_offset=None, bounds_check=NSLOT - 1,
                            oob_is_err=False).then_inc(dispatched[tr.b], 16)

            attention_steps(pool, step)

            pool.wait_ge(S.zeroed, 16 * NT)
            with pool.Fori(0, NE // 2) as i:
                for c in range(2):
                    e = 2 * i + c
                    pool.wait_ge(S.yidx_ready, e + 1)
                    pool.wait_ge(S.y_evac, 2 * e + 2)
                    hold(pool)
                    for j in range(ST):
                        g.indirect_dma_start(
                            out=pairs_d, out_offset=bass.IndirectOffsetOnAxis(ap=yidx[:, c, j:j + 1], axis=0),
                            in_=yout[:, c, j, :], in_offset=None, bounds_check=N * TOPK - 1,
                            oob_is_err=False).then_inc(y_sent[c], 16)

        @block.scalar
        def _(act):
            a = nc.scalar
            act.dma_start(cent[0:NGR, :], group_c).then_inc(S.cent_loaded, 16)
            act.dma_start(cent[NGR:NGR + NE, :], expert_c).then_inc(S.cent_loaded, 16)
            act.dma_start(wqkv[:, :], w_qkv).then_inc(S.w_loaded, 16)
            act.dma_start(wout[:, :], w_out).then_inc(S.w_loaded, 16)
            act.dma_start(bias_b[:, :], bias.rearrange("(o e) -> o e", o=1).broadcast_to([P, NE]))\
               .then_inc(S.w_loaded, 16)
            act.dma_start(sgw[:, :], s_g).then_inc(S.w_loaded, 16)
            act.dma_start(suw[:, :], s_u).then_inc(S.w_loaded, 16)
            act.dma_start(sdw[:, :, :], s_d.rearrange("(c p) n -> p c n", c=2)).then_inc(S.w_loaded, 16)
            act.wait_ge(S.cent_loaded, 32)
            a.activation(cent_sq[:, :], cent[:, :], ACT.Square, accum_out=cent_n[:, 0:1]).then_inc(S.cent_sum, 1)

            def step(tau, tn, tf, tp, ts, tw, tr):
                if tr is not None:
                    act.wait_ge(S.xfT_done, tr.n + 1)
                    wait(act, S.router_done, tr.n - 1)
                    wait(act, S.xfT_kept, tr.n - 1)
                    a.copy(xfT[:, tr.b], bank[4][:, 3 * D:3 * D + P]).then_inc(S.xfT_evac, 1)
                if tf is not None:
                    act.wait_ge(S.xnT_done, tf.n + 1)
                    wait(act, S.qkv_done, tf.n - 1)
                    a.copy(xnT[:, tf.b], bank[5][:, 0:P]).then_inc(S.xnT_evac, 1)
                if tw is not None:
                    act.wait_ge(S.oT_done, tw.n + 1)
                    wait(act, S.wout_done, tw.n - 1)
                    a.copy(oT[:, tw.b], bank[3][:, 0:P]).then_inc(S.oT_evac, 1)
                if tf is not None:
                    b = tf.b
                    act.wait_ge(S.rope_r, tf.n + 1)
                    wait(act, S.qkT_done, 2 * (tf.n - 1))
                    wait(act, S.split_lo, 2 * (tf.n - 1))
                    r = rr[:, b].rearrange("p (w h d) -> p w h d", w=2, h=H)
                    for w, part in enumerate((Q_HI, K_HI)):
                        a.copy(qk[:, b, w, :, part, :], r[:, w].unsqueeze(2).broadcast_to([P, H, 3, DH]))\
                         .then_inc(S.split_hi, 1)
                if ts is not None:
                    wait(act, S.pv_done, ts.n - 1)
                    for u in range(NU):
                        act.wait_ge(S.p2_scores, NU * ts.n + (u + 1))
                        a.activation(pt[:, ts.b, u], bank[2 + u % 2][:, :], ACT.Exp, scale=QK_SCALE)\
                         .then_inc(S.exp_done, 1)
                if tr is not None:
                    act.wait_ge(S.route, 12 * tr.n + 10)
                    wait(act, S.gate_done, 2 * (tr.n - 1))
                    a.activation(ex4[:, tr.b], ed4[:, tr.b], ACT.Exp, accum_out=exs[:, tr.b]).then_inc(S.gate_exp, 1)
                if ts is not None:
                    act.wait_ge(S.pv_done, ts.n + 1)
                    wait(act, S.pvT_done, ts.n - 1)
                    a.copy(pvT[:, ts.b], bank[7][:, :]).then_inc(S.pv_evac, 1)
                if tf is not None:
                    v = bank[4][:, 2 * D:3 * D].rearrange("p (h d) -> p h d", h=H)
                    act.wait_ge(S.rope_ab, 3 * tf.n + 3)
                    wait(act, S.pv_done, tf.n - 1)
                    wait(act, S.v_prev, tf.n - 1)
                    a.copy(v_cur[:, b, :, 0:DH], v).then_inc(S.v_evac, 1)
                    a.copy(v_mix[WIN:P, b, :, 0:DH], v[0:WIN]).then_inc(S.v_evac, 1)
                    if not isinstance(tf.n, int) or tf.n:
                        act.wait_ge(S.v_evac, 2 * tf.n)
                        a.copy(v_mix[0:WIN, b, :, 0:DH], v_cur[WIN:P, 1 - b, :, 0:DH]).then_inc(S.v_prev, 1)
                    wait(act, S.p2_scores, NU * (tf.n - 1))
                    act.wait_ge(S.qkT_done, 2 * tf.n + 1)
                    a.copy(qT[:, b], bank[5][:, :].bitcast(BF16).rearrange("p (g t) -> p g t", g=NG))\
                     .then_inc(S.qT_evac, 1)
                    act.wait_ge(S.qkT_done, 2 * tf.n + 2)
                    wait(act, S.k_prev, tf.n - 1)
                    a.copy(kT[:, b, :, WIN:SPAN], bank[6][:, :].bitcast(BF16).rearrange("p (g t) -> p g t", g=NG))\
                     .then_inc(S.kT_evac, 1)

            attention_steps(act, step)

            def shared_step(m, _):
                if m is not None:
                    for h in range(2):
                        act.wait_ge(S.sh_gu, 4 * m.n + (2 * h + 1))
                        wait(act, S.sh_down, m.n - 1)
                        a.activation(sact[:, m.b, h], bank[h][:, :], ACT.Silu).then_inc(S.sh_act, 1)

            lagged_steps(act, shared_step, N // 512, False)

            def expert_step(_, e, ed):
                def silu(ch):
                    for h in range(2):
                        act.wait_ge(S.gu_done, 8 * e.n + (4 * ch + 2 * h + 1))
                        a.activation(hact[:, e.b, h, ch * CH:(ch + 1) * CH], bank[2 + h][:, 0:CH], ACT.Silu)\
                         .then_inc(S.h_act, 1)

                if e is not None:
                    wait(act, S.down_done, e.n - 1)
                    silu(0)
                if ed is not None:
                    act.wait_ge(S.down_done, ed.n + 1)
                    wait(act, y_sent[ed.b], 16 * ST * ed.half)
                    a.copy(yout[:, ed.b, 0:4], bank[6][:, :].rearrange("p (j d) -> p j d", d=D))\
                     .then_inc(S.y_evac, 1)
                    a.copy(yout[:, ed.b, 4:ST], bank[7][:, 0:D].rearrange("p (j d) -> p j d", d=D))\
                     .then_inc(S.y_evac, 1)
                if e is not None:
                    silu(1)

            lagged_steps(act, expert_step, NE, True)

            with act.Fori(0, NT) as t:
                act.wait_ge(S.comb_step, TOPK * (t + 1))
                act.dma_start(out_v[:, bass.ds(t, 1), :], x_all[:, bass.ds(t, 1), :]).then_inc(S.stored, 16)
            act.wait_ge(S.stored, 16 * NT)

        @block.tensor
        def _(pe):
            mm = nc.tensor.matmul
            pe.wait_ge(S.casts, 15)
            pe.wait_ge(S.cent_unit, 1)
            nc.tensor.transpose(bank[0][:, 0:NGR + NE], cent_sq[:, :], ident[0:NGR + NE, 0:NGR + NE])\
              .then_inc(S.centT_done, 1)
            pe.wait_ge(S.w_loaded, 16 * 6)
            pe.wait_ge(S.centT_evac, 1)

            def step(tau, tn, tf, tp, ts, tw, tr):
                def first_scores(u):
                    s, g4 = u % NS, u // NS * 4
                    bk = bank[u % 2]
                    wait(pe, S.p1_reduced, NU * tp.n + (u - 1) if not isinstance(tp.n, int) or tp.n else u - 1)
                    if u == 1:
                        wait(pe, S.mT_evac, tp.n)
                    mm(bk[:, :].rearrange("p (c j) -> p c j", c=4), ident_b[:, :],
                       maskq_b[:, :].unsqueeze(1).broadcast_to([P, 4, P]), start=True, stop=False,
                       skip_group_check=True)
                    rows = slice(STRIP * s, STRIP * (s + 1))
                    for hb in range(2):
                        for c in range(4):
                            last = mm(bk[hb * WIN:(hb + 1) * WIN, c * P:(c + 1) * P],
                                      qT[rows, tp.b, g4 + c, hb * WIN:(hb + 1) * WIN],
                                      kT[rows, tp.b, g4 + c, hb * WIN:hb * WIN + P], start=False, stop=(c == 3),
                                      skip_group_check=True)
                    last.then_inc(S.p1_scores, 1)

                def second_scores(u):
                    s, g4 = u % NS, u // NS * 4
                    bk = bank[2 + u % 2]
                    wait(pe, S.exp_done, NU * ts.n + (u - 1) if not isinstance(ts.n, int) or ts.n else u - 1)
                    for c in range(4):
                        mm(bk[:, c * P:(c + 1) * P], comb_st[0:WIN + 3 * H, NS * (g4 + c) + s, :],
                           comb_mv[0:WIN + 3 * H, ts.b, :], start=(c == 0), stop=False, skip_group_check=True)
                    rows = slice(STRIP * s, STRIP * (s + 1))
                    for c in range(4):
                        for hb in range(2):
                            at = c * P + hb * WIN
                            last = mm(bk[:, at:at + WIN], kT[rows, ts.b, g4 + c, hb * WIN:hb * WIN + P],
                                      qT[rows, ts.b, g4 + c, hb * WIN:(hb + 1) * WIN], start=False,
                                      stop=(c == 3 and hb == 1), skip_group_check=True)
                    last.then_inc(S.p2_scores, 1)

                def weighted_values(u):
                    pe.wait_ge(S.exp_done, NU * ts.n + (u + 1))
                    for c in range(4):
                        h = NS * (u // NS * 4 + c) + u % NS
                        for hb in range(2):
                            vals = (v_cur if hb else v_mix)[:, ts.b, h, :]
                            at = c * P + hb * WIN
                            to = h // 4 * P + hb * WIN
                            last = mm(bank[7][32 * (h % 4):32 * (h % 4 + 1), to:to + WIN], vals,
                                      pt[:, ts.b, u, at:at + WIN], start=True, stop=True)
                    return last

                if tw is not None:
                    pe.wait_ge(S.pv_evac, tw.n + 1)
                    pe.wait_ge(S.exp_done, NU * tw.n + NU)
                    for q in range(4):
                        last = nc.tensor.transpose(bank[2][:, q * P:(q + 1) * P], pvT[:, tw.b, q * P:(q + 1) * P],
                                                   ident[:, :])
                    last.then_inc(S.pvT_done, 1)
                if tr is not None:
                    pe.wait_ge(S.xf_ready, tr.n + 1)
                    pe.wait_ge(S.v_evac, min(2 * (tr.n + 4), 2 * NT) if isinstance(tr.n, int) else 2 * (tr.n + 4))
                    nc.tensor.transpose(bank[4][:, 3 * D:3 * D + P], xfe[:, tr.b, 0, 0:D], ident[:, :])\
                      .then_inc(S.xfT_done, 1)
                if tf is not None:
                    pe.wait_ge(S.xn_ready, tf.n + 1)
                    wait(pe, S.qT_evac, tf.n)
                    nc.tensor.transpose(bank[5][:, 0:P], xn[:, tf.b], ident[:, :]).then_inc(S.xnT_done, 1)
                if tp is not None:
                    pe.wait_ge(S.qT_evac, tp.n + 1)
                    pe.wait_ge(S.kT_evac, tp.n + 1)
                    wait(pe, S.k_prev, tp.n)
                    first_scores(0)
                if tr is not None:
                    pe.wait_ge(S.xfT_evac, tr.n + 1)
                    pe.wait_ge(S.kT_evac, min(tr.n + 4, NT) if isinstance(tr.n, int) else tr.n + 4)
                    wait(pe, S.pos_read, tr.n)
                    mm(bank[6][:, 0:NGR + NE], xfT[:, tr.b], centT[:, :], start=True, stop=True)\
                      .then_inc(S.router_done, 1)
                if tf is not None:
                    pe.wait_ge(S.xnT_evac, tf.n + 1)
                    wait(pe, S.v_evac, 2 * tf.n)
                    if tr is not None:
                        pe.wait_ge(S.xfT_evac, tr.n + 1)
                    mm(bank[4][:, 0:3 * D], xnT[:, tf.b], wqkv[:, :], start=True, stop=True).then_inc(S.qkv_done, 1)
                if tp is not None:
                    first_scores(1)
                if tw is not None:
                    pe.wait_ge(S.onorm, tw.n + 1)
                    nc.tensor.transpose(bank[3][:, 0:P], on[:, tw.b], ident[:, :]).then_inc(S.oT_done, 1)
                if tp is not None:
                    first_scores(2)
                if tw is not None:
                    pe.wait_ge(S.oT_evac, tw.n + 1)
                    mm(bank[3][:, P:2 * P], oT[:, tw.b], wout[:, :], start=True, stop=True).then_inc(S.wout_done, 1)
                if ts is not None:
                    pe.wait_ge(S.mT_evac, ts.n + 1)
                    wait(pe, S.onorm, ts.n)
                    second_scores(0)
                if tp is not None:
                    first_scores(3)
                if ts is not None:
                    wait(pe, S.x1_ready, ts.n)
                    second_scores(1)
                    second_scores(2)
                    second_scores(3)
                if tr is not None:
                    pe.wait_ge(S.sel_ready, tr.n + 1)
                    wait(pe, S.acc_ready, tr.n)
                    pe.wait_ge(S.sc_ready, tr.n + 1)
                    mm(bank[6][:, P:P + NE], before_b[:, :], msel[:, tr.b], start=True, stop=False)
                    mm(bank[6][:, P:P + NE], ones_b[:, :], macc[:, tr.b], start=False, stop=True)\
                      .then_inc(S.pos_done, 1)
                if ts is not None:
                    pe.wait_ge(S.v_evac, 2 * ts.n + 2)
                    wait(pe, S.v_prev, ts.n)
                    wait(pe, S.pv_evac, ts.n)
                    for u in range(NU):
                        last = weighted_values(u)
                    last.then_inc(S.pv_done, 1)
                if tp is not None:
                    pe.wait_ge(S.p1_reduced, NU * tp.n + NU)
                    pe.wait_ge(S.negm, 4 * tp.n + 4)
                    hold(pe)
                    nc.tensor.transpose(bank[1][:, :].bitcast(BF16)[0:3 * H, 0:P],
                                        mp[:, tp.b].rearrange("p c h -> p (c h)"), ident_b[:, :])\
                      .then_inc(S.mT_done, 1)
                if tf is not None:
                    pe.wait_ge(S.split_hi, 2 * tf.n + 2)
                    pe.wait_ge(S.split_lo, 2 * tf.n + 2)
                    for w in range(2):
                        if w and tr is not None:
                            pe.wait_ge(S.pos_read, tr.n + 1)
                        for gg in range(NG):
                            last = nc.tensor.transpose(
                                bank[5 + w][:, :].bitcast(BF16)[:, gg * P:(gg + 1) * P],
                                qk[:, tf.b, w, NS * gg:NS * (gg + 1)].rearrange("p h c d -> p (h c d)"),
                                ident_b[:, :])
                        last.then_inc(S.qkT_done, 1)

            attention_steps(pe, step)

            pe.wait_ge(S.mT_evac, NT)
            pe.wait_ge(S.v_evac, 2 * NT)
            pe.wait_ge(S.pos_read, NT)
            pe.wait_ge(S.xfT_kept, NT)
            pe.wait_ge(S.x1_ready, NT)

            def shared_step(m, md):
                if m is not None:
                    for h in range(2):
                        cols = slice(h * P, (h + 1) * P)
                        wait(pe, S.sh_act, 2 * m.n + (h - 1) if not isinstance(m.n, int) or m.n else 0)
                        mm(bank[h][:, :], sgw[:, cols], xfT_all[:, bass.ts(m.n, 512)], start=True, stop=True)\
                          .then_inc(S.sh_gu, 1)
                        wait(pe, S.sh_mul, 2 * m.n + (h - 1) if not isinstance(m.n, int) or m.n else 0)
                        mm(bank[2 + h][:, :], suw[:, cols], xfT_all[:, bass.ts(m.n, 512)], start=True, stop=True)\
                          .then_inc(S.sh_gu, 1)
                if md is not None:
                    pe.wait_ge(S.sh_mul, 2 * md.n + 2)
                    wait(pe, S.sh_added, md.n - 1)
                    for j in range(4):
                        for h in range(2):
                            last = mm(bank[4 + md.b][:, j * D:(j + 1) * D], sact[:, md.b, h, j * P:(j + 1) * P],
                                      sdw[:, h, :], start=(h == 0), stop=(h == 1))
                    last.then_inc(S.sh_down, 1)

            lagged_steps(pe, shared_step, N // 512, False)
            pe.wait_ge(S.sh_added, N // 512)

            def expert_step(en, e, ed):
                def gate_up(ch):
                    for h in range(2):
                        for w in range(2):
                            wait(pe, (S.h_act, S.h_mul)[w],
                                 4 * e.n + (2 * ch + h - 1) if not isinstance(e.n, int) or e.n else 2 * ch + h - 1)
                            mm(bank[2 + 2 * w + h][:, 0:CH], wgu[:, e.b, w, h * P:(h + 1) * P],
                               xgT[:, e.b, ch * CH:(ch + 1) * CH], start=True, stop=True).then_inc(S.gu_done, 1)

                if e is not None:
                    pe.wait_ge(wgu_arrived[e.b], 32 * (e.half + 1))
                    pe.wait_ge(S.xgT_evac, 2 * e.n + 2)
                    gate_up(0)
                if ed is not None:
                    pe.wait_ge(wdn_arrived[ed.b], 16 * (ed.half + 1))
                    pe.wait_ge(S.h_mul, 4 * ed.n + 4)
                    wait(pe, S.y_evac, 2 * ed.n)
                    for j in range(ST):
                        for h in range(2):
                            last = mm(bank[6 + j // 4][:, j % 4 * D:(j % 4 + 1) * D],
                                      hact[:, ed.b, h, j * P:(j + 1) * P], wdn[:, ed.b, h, :],
                                      start=(h == 0), stop=(h == 1))
                    last.then_inc(S.down_done, 1)
                if e is not None:
                    gate_up(1)
                if en is not None:
                    pe.wait_ge(xg_arrived[en.b], 16 * (en.half + 1))
                    wait(pe, S.xgT_evac, 2 * en.n)
                    for j in range(ST):
                        tt = nc.tensor.transpose(bank[j // 4][:, j % 4 * P:(j % 4 + 1) * P], xg[:, en.b, j, 0:D],
                                                 ident[:, :])
                        if j == 3 or j == ST - 1:
                            tt.then_inc(S.xgT_done, 1)

            lagged_steps(pe, expert_step, NE, True)

        @block.vector
        def _(dve):
            v = nc.vector
            dve.wait_ge(S.const_loaded, 16)
            casts = [
                v.tensor_copy(ident_b[:, :], ident),
                v.tensor_copy(before_b[:, :], field("before")),
                v.memset(ones_b[:, :], 1.0),
                v.tensor_copy(maskq_b[:, :], field("maskq")),
                v.tensor_copy(comb_st[0:WIN], field("comb")[0:WIN].unsqueeze(1).broadcast_to([WIN, H, P])),
                v.tensor_copy(comb_st[WIN:WIN + 3 * H],
                              field("head_rows")[WIN:WIN + 3 * H].unsqueeze(2).broadcast_to([3 * H, H, P])),
                v.tensor_copy(comb_mv[0:WIN], field("eye2")[0:WIN].unsqueeze(1).broadcast_to([WIN, 2, P])),
                v.memset(qk[:, :, :, :, :, :], 0.0),
                v.memset(v_cur[:, :, :, :], 0.0),
                v.memset(v_mix[:, :, :, :], 0.0),
                v.memset(macc[:, 0], 0.0),
                v.tensor_copy(kT[:, 0, :, 0:WIN],
                              pen[:, 0:1].unsqueeze(2).broadcast_to([P, NG, WIN])),
            ]
            for ins in casts:
                ins.then_inc(S.casts, 1)
            dve.wait_ge(S.casts, 10)
            v.memset(qk[:, :, 0, :, 7, 0:1], 1.0).then_inc(S.casts, 1)
            v.memset(v_cur[:, :, :, DH:DH + 1], 1.0).then_inc(S.casts, 1)
            v.memset(v_mix[:, :, :, DH:DH + 1], 1.0).then_inc(S.casts, 1)
            dve.wait_ge(S.cent_len, 3)
            v.tensor_scalar(cent_sq[:, :], cent[:, :], cent_n[:, 2:3], None, ALU.mult).then_inc(S.cent_unit, 1)
            dve.wait_ge(S.centT_done, 1)
            v.tensor_copy(centT[:, :], bank[0][:, 0:NGR + NE]).then_inc(S.centT_evac, 1)
            dve.wait_ge(S.x_loaded, 16)
            dve.wait_ge(S.w_loaded, 16 * 6)

            def step(tau, tn, tf, tp, ts, tw, tr):
                def maxima(u):
                    m = mx[:, tp.b].rearrange("p (g s) -> p g s", s=NS)
                    s, g4 = u % NS, u // NS * 4
                    dve.wait_ge(S.p1_scores, NU * tp.n + (u + 1))
                    v.tensor_reduce(m[:, g4:g4 + 4, s], bank[u % 2][:, :].rearrange("p (c j) -> p c j", c=4),
                                    AX.X, ALU.max).then_inc(S.p1_reduced, 1)

                R = 12
                by_group = lambda ap: ap.rearrange("p (g e) -> p g e", g=NGR)
                row = lambda t: x_all[:, bass.ds(t.n, 1), :].rearrange("p o d -> p (o d)")

                if tw is not None:
                    dve.wait_ge(S.pvT_done, tw.n + 1)
                    wait(dve, S.oT_done, tw.n - 1)
                    wait(dve, S.onorm, tw.n)
                    pv = bank[2][:, :].rearrange("p (h d) -> p h d", h=H)
                    v.reciprocal(rec[:, :], pv[:, :, DH]).then_inc(S.recip, 1)
                if tn is not None:
                    v.bn_stats(st1[:, :], row(tn)).then_inc(S.ln1, 1)
                if tw is not None:
                    dve.wait_ge(S.recip, tw.n + 1)
                    v.tensor_tensor(on[:, tw.b].rearrange("p (h d) -> p h d", h=H), pv[:, :, 0:DH],
                                    rec[:, :].unsqueeze(2).broadcast_to([P, H, DH]), ALU.mult).then_inc(S.onorm, 1)
                if tn is not None:
                    dve.wait_ge(S.ln1, 3 * tn.n + 1)
                    hold(dve)
                    v.bn_aggr(mv1[:, tn.b], st1[:, :]).then_inc(S.ln1, 1)
                if tp is not None:
                    maxima(0)
                if tn is not None:
                    dve.wait_ge(S.ln1, 3 * tn.n + 2)
                    v.tensor_scalar(pin[:, tn.b, 0:1], mv1[:, tn.b, 1:2], EPS, None, ALU.add).then_inc(S.ln1, 1)
                if tr is not None:
                    n = tr.n
                    dve.wait_ge(S.router_done, n + 1)
                    v.tensor_scalar(sc[:, :], bank[6][:, 0:NGR + NE], pout[:, tr.b, 2:3], None, ALU.mult)\
                     .then_inc(S.sc_ready, 1)
                if tf is not None:
                    dve.wait_ge(S.qkv_done, tf.n + 1)
                    wait(dve, S.rope_r, tf.n)
                    z = bank[4][:, 0:2 * D].rearrange("p (h c i) -> p h c i", c=2, i=HALF)
                    zb = rb[:, :].rearrange("p (h c i) -> p h c i", c=2, i=HALF)
                    ct = cos[:, bass.ds(tf.n, 1), :].broadcast_to([P, 4 * H, HALF])
                    stn = sin[:, bass.ds(tf.n, 1), :].broadcast_to([P, 2 * H, HALF])
                    v.tensor_tensor(ra[:, :].rearrange("p (m i) -> p m i", i=HALF),
                                    bank[4][:, 0:2 * D].rearrange("p (m i) -> p m i", i=HALF), ct,
                                    ALU.mult).then_inc(S.rope_ab, 1)
                if tr is not None:
                    dve.wait_ge(S.sc_ready, n + 1)
                    v.tensor_tensor(es[:, :], sc[:, NGR:NGR + NE], bias_b[:, :], ALU.add).then_inc(S.route, 1)
                    v.max(gm8[:, :], sc[:, 0:NGR]).then_inc(S.route, 1)
                if tf is not None:
                    v.scalar_tensor_tensor(zb[:, :, 0], z[:, :, 1], -1.0, stn, ALU.mult, ALU.mult)\
                     .then_inc(S.rope_ab, 1)
                if tr is not None:
                    dve.wait_ge(S.route, R * n + 2)
                    hold(dve)
                    v.max_index(gi8[:, :], gm8[:, :], sc[:, 0:NGR]).then_inc(S.route, 1)
                if tf is not None:
                    v.tensor_tensor(zb[:, :, 1], z[:, :, 0], stn, ALU.mult).then_inc(S.rope_ab, 1)
                if tr is not None:
                    dve.wait_ge(S.route, R * n + 3)
                    v.tensor_tensor(geq[:, :, :], numbers[:, 0:NGR].unsqueeze(2).broadcast_to([P, NGR, TOPG]),
                                    gi8[:, 0:TOPG].unsqueeze(1).broadcast_to([P, NGR, TOPG]), ALU.is_equal)\
                     .then_inc(S.route, 1)
                if tp is not None:
                    maxima(1)
                if tr is not None:
                    dve.wait_ge(S.route, R * n + 4)
                    v.tensor_reduce(gsel[:, :], geq[:, :, :], AX.X, ALU.add).then_inc(S.route, 1)
                if tw is not None:
                    dve.wait_ge(S.wout_done, tw.n + 1)
                    v.tensor_tensor(row(tw), row(tw), bank[3][:, P:2 * P], ALU.add).then_inc(S.x1_ready, 1)
                if tr is not None:
                    dve.wait_ge(S.route, R * n + 5)
                    v.tensor_scalar(gpen[:, :], gsel[:, :], 1e9, -1e9, ALU.mult, ALU.add).then_inc(S.route, 1)
                    v.tensor_tensor(by_group(es2[:, :]), by_group(es[:, :]),
                                    gsel[:, :].unsqueeze(2).broadcast_to([P, NGR, EPG]), ALU.mult)\
                     .then_inc(S.route, 1)
                if tw is not None:
                    dve.wait_ge(S.x1_ready, tw.n + 1)
                    hold(dve)
                    v.bn_stats(st2[:, :], row(tw)).then_inc(S.ln2, 1)
                if tr is not None:
                    dve.wait_ge(S.route, R * n + 7)
                    v.tensor_tensor(by_group(es[:, :]), by_group(es2[:, :]),
                                    gpen[:, :].unsqueeze(2).broadcast_to([P, NGR, EPG]), ALU.add)\
                     .then_inc(S.route, 1)
                if tw is not None:
                    dve.wait_ge(S.ln2, 6 * tw.n + 1)
                    hold(dve)
                    v.bn_aggr(mv2[:, tw.b], st2[:, :]).then_inc(S.ln2, 1)
                if tr is not None:
                    dve.wait_ge(S.route, R * n + 8)
                    hold(dve)
                    v.max(em8[:, :], es[:, :]).then_inc(S.route, 1)
                if tw is not None:
                    c = tw.b
                    dve.wait_ge(S.ln2, 6 * tw.n + 2)
                    v.tensor_scalar(pin[:, c, 1:2], mv2[:, tw.b, 1:2], EPS, None, ALU.add).then_inc(S.ln2, 1)
                if tp is not None:
                    maxima(2)
                if tr is not None:
                    dve.wait_ge(S.route, R * n + 9)
                    wait(dve, S.gate_exp, n - 1)
                    hold(dve)
                    v.tensor_scalar(ed4[:, tr.b], em8[:, 0:TOPK], em8[:, 0:1], None, ALU.subtract)\
                     .then_inc(S.route, 1)
                    v.max_index(ei8[:, :], em8[:, :], es[:, :]).then_inc(S.route, 1)
                if tw is not None:
                    dve.wait_ge(S.ln2, 6 * tw.n + 3)
                    v.reciprocal(ve[:, 0:1], pin[:, c, 1:2]).then_inc(S.ln2, 1)
                if tr is not None:
                    dve.wait_ge(S.route, R * n + 11)
                    v.tensor_tensor(oh[:, :, :], numbers.unsqueeze(1).broadcast_to([P, TOPK, NE]),
                                    ei8[:, 0:TOPK].unsqueeze(2).broadcast_to([P, TOPK, NE]), ALU.is_equal)\
                     .then_inc(S.route, 1)
                if tw is not None:
                    dve.wait_ge(S.ln2, 6 * tw.n + 4)
                    v.tensor_scalar(ve[:, 1:2], ve[:, 0:1], mv2[:, tw.b, 1:2], float(D), ALU.mult, ALU.mult)\
                     .then_inc(S.ln2, 1)
                if tr is not None:
                    dve.wait_ge(S.route, R * n + 12)
                    wait(dve, S.pos_done, n - 1)
                    with nc.allow_low_precision("marks are 0 or 1"):
                        v.tensor_reduce(msel[:, tr.b], oh[:, :, :].rearrange("p k e -> p e k"), AX.X, ALU.add)\
                         .then_inc(S.sel_ready, 1)
                if tw is not None:
                    dve.wait_ge(S.ln2, 6 * tw.n + 5)
                    v.tensor_scalar(pin[:, c, 2:3], ve[:, 1:2], 1e-24, None, ALU.max).then_inc(S.ln2, 1)
                if tf is not None:
                    dve.wait_ge(S.split_hi, 2 * tf.n + 2)
                    wait(dve, S.split_lo, 2 * tf.n)
                    v.tensor_tensor(r1[:, :].rearrange("p (m d) -> p m d", d=DH),
                                    rr[:, tf.b].rearrange("p (m d) -> p m d", d=DH),
                                    qk[:, tf.b, :, :, 0, :].rearrange("p w h d -> p (w h) d"), ALU.subtract)\
                     .then_inc(S.split_rest, 1)
                if tp is not None:
                    maxima(3)
                mids = enumerate((Q_MID, K_MID))

                def middle():
                    w, part = next(mids)
                    src = r1[:, w * D:(w + 1) * D].rearrange("p (h d) -> p h d", h=H)
                    v.tensor_copy(qk[:, tf.b, w, :, part, :], src.unsqueeze(2).broadcast_to([P, H, 2, DH]))\
                     .then_inc(S.split_mid, 1)

                if tf is not None:
                    dve.wait_ge(S.split_rest, tf.n + 1)
                    middle()
                if tp is not None:
                    dve.wait_ge(S.p1_reduced, NU * tp.n + NU)
                    wait(dve, S.mT_done, tp.n - 1)
                    v.tensor_scalar(mp[:, tp.b, 0], mx[:, tp.b], -1.0, None, ALU.mult).then_inc(S.negm, 1)
                if tf is not None:
                    middle()
                if tp is not None:
                    dve.wait_ge(S.negm, 4 * tp.n + 1)
                    v.scalar_tensor_tensor(nm[:, :], mx[:, tp.b], -1.0, mp[:, tp.b, 0], ALU.mult,
                                           ALU.subtract).then_inc(S.negm, 1)
                if tr is not None:
                    dve.wait_ge(S.pos_done, n + 1)
                    v.tensor_tensor(macc[:, 1 - tr.b], macc[:, tr.b], msel[:, tr.b], ALU.add).then_inc(S.acc_ready, 1)
                if tp is not None:
                    dve.wait_ge(S.negm, 4 * tp.n + 2)
                    v.tensor_copy(mp[:, tp.b, 1], nm[:, :]).then_inc(S.negm, 1)
                if tr is not None:
                    v.tensor_tensor(ohp[:, :, :], oh[:, :, :],
                                    bank[6][:, P:P + NE].unsqueeze(1).broadcast_to([P, TOPK, NE]), ALU.mult)\
                     .then_inc(S.pos_read, 1)
                if tp is not None:
                    dve.wait_ge(S.negm, 4 * tp.n + 3)
                    v.tensor_tensor(mp[:, tp.b, 2], nm[:, :], mp[:, tp.b, 1], ALU.subtract).then_inc(S.negm, 1)
                if tr is not None:
                    dve.wait_ge(S.pos_read, n + 1)
                    v.tensor_reduce(posk[:, :], ohp[:, :, :], AX.X, ALU.add).then_inc(S.slots, 1)
                if tf is not None and (not isinstance(tf.n, int) or tf.n):
                    dve.wait_ge(S.kT_evac, tf.n)
                    wait(dve, S.p2_scores, NU * (tf.n - 1))
                    v.tensor_scalar(kT[:, tf.b, :, 0:WIN], kT[:, 1 - tf.b, :, P:SPAN],
                                    pen[:, bass.ds(tf.n, 1)], None, ALU.add).then_inc(S.k_prev, 1)
                if tn is not None:
                    dve.wait_ge(S.pow_done, tau + 2)
                    wait(dve, S.xnT_done, tn.n - 1)
                    v.tensor_scalar(xn[:, tn.b], row(tn), mv1[:, tn.b, 0:1], pout[:, tn.b, 0:1], ALU.subtract,
                                    ALU.mult).then_inc(S.xn_ready, 1)
                if tr is not None:
                    dve.wait_ge(S.slots, 4 * n + 1)
                    v.tensor_scalar(keep[:, :], posk[:, :], float(cap), None, ALU.is_lt).then_inc(S.slots, 1)
                    v.scalar_tensor_tensor(slotf[:, :], ei8[:, 0:TOPK], float(cap), posk[:, :], ALU.mult,
                                           ALU.add).then_inc(S.slots, 1)
                if tw is not None:
                    dve.wait_ge(S.pow_done, tau + 2)
                    wait(dve, dispatched[tw.b], 16 * TOPK * tw.half)
                    wait(dve, S.xfT_done, tw.n - 1)
                    v.tensor_scalar(xfe[:, tw.b, :, 0:D], x_all[:, bass.ds(tw.n, 1), :].broadcast_to([P, TOPK, D]),
                                    mv2[:, tw.b, 0:1], pout[:, tw.b, 1:2], ALU.subtract, ALU.mult)\
                     .then_inc(S.xf_ready, 1)
                if tr is not None:
                    dve.wait_ge(S.slots, 4 * n + 3)
                    v.scalar_tensor_tensor(slotf2[:, :], keep[:, :], -OOB, slotf[:, :], ALU.mult, ALU.add)\
                     .then_inc(S.slots, 1)
                    dve.wait_ge(S.gate_exp, n + 1)
                    v.reciprocal(exr[:, :], exs[:, tr.b]).then_inc(S.gate_done, 1)
                if tp is not None:
                    dve.wait_ge(S.mT_done, tp.n + 1)
                    wait(dve, S.p2_scores, NU * (tp.n - 1))
                    v.tensor_copy(comb_mv[WIN:WIN + 3 * H, tp.b, :], bank[1][:, :].bitcast(BF16)[0:3 * H, 0:P])\
                     .then_inc(S.mT_evac, 1)
                if tr is not None:
                    dve.wait_ge(S.slots, 4 * n + 4)
                    wait(dve, dispatched[tr.b], 16 * TOPK * tr.half)
                    v.tensor_scalar(sidx[:, tr.b], slotf2[:, :], OOB, None, ALU.add).then_inc(S.slot_ready, 1)
                    dve.wait_ge(S.gate_done, 2 * n + 1)
                    v.scalar_tensor_tensor(gates[:, bass.ds(n, 1), :].rearrange("p o k -> p (o k)"), ex4[:, tr.b],
                                           exr[:, :], keep[:, :], ALU.mult, ALU.mult).then_inc(S.gate_done, 1)

            attention_steps(dve, step)

            def shared_step(m, md):
                if m is not None:
                    for h in range(2):
                        dve.wait_ge(S.sh_act, 2 * m.n + (h + 1))
                        dve.wait_ge(S.sh_gu, 4 * m.n + (2 * h + 2))
                        v.tensor_tensor(sact[:, m.b, h], sact[:, m.b, h], bank[2 + h][:, :], ALU.mult)\
                         .then_inc(S.sh_mul, 1)
                if md is not None:
                    dve.wait_ge(S.sh_down, md.n + 1)
                    xs = x_all[:, bass.ds(4 * md.n, 4), :]
                    v.tensor_tensor(xs, xs, bank[4 + md.b][:, :].rearrange("p (t d) -> p t d", d=D), ALU.add)\
                     .then_inc(S.sh_added, 1)

            lagged_steps(dve, shared_step, N // 512, False)

            def expert_step(en, e, ed):
                def times_up(ch):
                    for h in range(2):
                        dve.wait_ge(S.h_act, 4 * e.n + (2 * ch + h + 1))
                        dve.wait_ge(S.gu_done, 8 * e.n + (4 * ch + 2 * h + 2))
                        hs = hact[:, e.b, h, ch * CH:(ch + 1) * CH]
                        v.tensor_tensor(hs, hs, bank[4 + h][:, 0:CH], ALU.mult).then_inc(S.h_mul, 1)

                if e is not None:
                    times_up(0)
                if ed is not None:
                    dve.wait_ge(S.ypair_ready, ed.n + 1)
                    wait(dve, y_sent[ed.b], 16 * ST * ed.half)
                    v.tensor_copy(yidx[:, ed.b], ypair[:, ed.b]).then_inc(S.yidx_ready, 1)
                if e is not None:
                    times_up(1)
                if en is not None:
                    dve.wait_ge(xg_arrived[en.b], 16 * (en.half + 1))
                    wait(dve, S.yidx_ready, en.n - 1)
                    v.tensor_copy(ypair[:, en.b], xg[:, en.b, :, D]).then_inc(S.ypair_ready, 1)
                    wait(dve, S.gu_done, 8 * (en.n - 1))
                    dve.wait_ge(S.xgT_done, 2 * en.n + 1)
                    v.tensor_copy(xgT[:, en.b, 0:4 * P], bank[0][:, :]).then_inc(S.xgT_evac, 1)
                    dve.wait_ge(S.xgT_done, 2 * en.n + 2)
                    v.tensor_copy(xgT[:, en.b, 4 * P:cap], bank[1][:, 0:cap - 4 * P]).then_inc(S.xgT_evac, 1)

            lagged_steps(dve, expert_step, NE, True)

            dve.wait_ge(S.sh_added, N // 512)
            with dve.Fori(0, NT // 4) as i:
                for c in range(4):
                    t = 4 * i + c
                    xt = x_all[:, bass.ds(t, 1), :].rearrange("p o d -> p (o d)")
                    dve.wait_ge(r_arrived[c], 16 * (i + 1))
                    for k in range(TOPK):
                        if k:
                            dve.wait_ge(S.comb_step, TOPK * t + k)
                        gk = gates[:, bass.ds(t, 1), k:k + 1].rearrange("p o k -> p (o k)")
                        v.scalar_tensor_tensor(xt, rload[:, c, k], gk, xt, ALU.mult, ALU.add)\
                         .then_inc(S.comb_step, 1)


_INS = ["L0_attn_x", "L0_attn_Wqkv", "L0_attn_Wout", "L0_ffn_group_centroids", "L0_ffn_expert_centroids",
        "L0_ffn_bias", "L0_ffn_wg", "L0_ffn_wu", "L0_ffn_wd", "L0_ffn_sg", "L0_ffn_su", "L0_ffn_sd"]


def kernel(**inputs):
    import numpy as _np
    import concourse.bacc as _bacc
    from concourse import mybir as _mybir
    from concourse.bass_utils import run_bass_kernel_spmd as _run

    nc = _bacc.Bacc("TRN2", target_bir_lowering=False, num_devices=1)
    arrays, args = {}, []
    for name in _INS:
        a = _np.ascontiguousarray(inputs[name])
        arrays[f"in_{name}_dram"] = a
        args.append(nc.dram_tensor(f"in_{name}_dram", a.shape, _mybir.dt.from_np(a.dtype), kind="ExternalInput").ap())
    shape = inputs["L0_attn_x"].shape
    const, where, cap = constants(shape[0] * shape[1], shape[1])
    arrays["constants_dram"] = const
    args.append(nc.dram_tensor("constants_dram", const.shape, _mybir.dt.float32, kind="ExternalInput").ap())
    args.append(nc.dram_tensor("out_0_dram", shape, _mybir.dt.float32, kind="ExternalOutput").ap())
    block_kernel(nc, *args, where, cap)
    r = _run(nc, [arrays], core_ids=[0])
    return r.results[0]["out_0_dram"]
```

```python
from collections import namedtuple
from contextlib import ExitStack

import concourse.bass as bass
from concourse import mybir

F32 = mybir.dt.float32
F32R = mybir.dt.float32r
BF16 = mybir.dt.bfloat16
U32 = mybir.dt.uint32
ALU = mybir.AluOpType
ACT = mybir.ActivationFunctionType
AX = mybir.AxisListType

P = 128
H, DH, WIN = 16, 8, 64
HALF = DH // 2
STRIP = 64
NS = P // STRIP
NG = H // NS
Q_HI, Q_MID, Q_LO = slice(0, 7, 3), slice(1, 5, 3), slice(2, 3)
K_HI, K_MID, K_LO = slice(0, 3), slice(3, 5), slice(6, 7)
PEN_ROW = 7 * DH
NU = H // 4
NEG = -1e30
NE, NGR, TOPG, TOPK = 32, 8, 4, 4
EPG = NE // NGR
FF = 256
EPS = 1e-5

Tile = namedtuple("Tile", "n half b")


def tile_of(half, b):
    return Tile(2 * half + b, half, b)


def constants(N, T):
    import numpy as np

    cap = max(1, int(N / NE * TOPK * 1.25))
    p = np.arange(P)
    theta = (1.0 / np.float32(10000.0) ** (np.arange(HALF, dtype=np.float32) / np.float32(HALF))).astype(np.float32)
    pos = (np.arange(N) % T).astype(np.float32)
    freq = (pos[:, None] * theta[None, :]).astype(np.float32)
    per_tile = lambda a: a.reshape(N // P, P, HALF).transpose(1, 0, 2).reshape(P, -1)
    pen = np.zeros((P, N // P), np.float32)
    pen[PEN_ROW::STRIP, ::T // P] = NEG
    kb = np.arange(P)[None, :]
    qb = np.arange(WIN)[:, None]
    comb = np.zeros((P, P), np.float32)
    comb[:WIN] = np.where((kb > qb) & (kb <= qb + WIN), 0.0, NEG)
    head_rows = np.zeros((P, H), np.float32)
    for part in range(3):
        head_rows[WIN + part * H:WIN + (part + 1) * H] = np.eye(H)
    fields = {
        "cos": per_tile(np.cos(freq)),
        "sin": per_tile(np.sin(freq)),
        "pen": pen,
        "ident": np.eye(P),
        "before": (p[:, None] < p[None, :]),
        "maskq": np.where((kb > p[:, None] % WIN) & (kb <= p[:, None] % WIN + WIN), 0.0, NEG),
        "comb": comb,
        "head_rows": head_rows,
        "eye2": np.concatenate([np.eye(P)[:, :WIN], np.eye(P)[:, :WIN]], 1),
        "numbers": np.tile(np.arange(NE), (P, 1)),
        "pair": ((np.arange(N // P)[None, :, None] * P + p[:, None, None]) * TOPK + np.arange(TOPK)).reshape(P, -1),
    }
    at, where = 0, {}
    for name, a in fields.items():
        where[name] = (at, a.shape[1])
        at += a.shape[1]
    return np.concatenate([np.asarray(a, np.float32) for a in fields.values()], 1), where, cap


def block_kernel(nc, x, w_qkv, w_out, group_c, expert_c, bias, w_g, w_u, w_d, s_g, s_u, s_d, const, out, where, cap):
    BT, T, D = x.shape
    N = BT * T
    NT = N // P
    NSLOT = NE * cap
    ST = cap // P
    SPAN = P + WIN
    ROW = D + 1
    OOB = float(1 << 20)
    QK_SCALE = float(DH) ** -0.5
    CH = cap // 2
    SHARED_EARLY = 2
    NR = 8
    CSTEPS = 5
    COMB_EARLY = 4 * (N // 512 - SHARED_EARLY - 2)
    assert D == P and cap % P == 0 and NT % 2 == 0 and H * DH == D

    x_v = x.rearrange("b (t p) d -> p (b t) d", p=P)
    out_v = out.rearrange("b (t p) d -> p (b t) d", p=P)
    slots_d = nc.dram_tensor("expert_slots", [NSLOT, ROW], F32, kind="Internal").ap()
    pairs_d = nc.dram_tensor("pair_results", [N * TOPK, D], F32, kind="Internal").ap()
    slots_v = slots_d.rearrange("(e p j) c -> e p (j c)", p=P, j=ST)
    pairs_v = pairs_d.rearrange("(t p k) d -> t p (k d)", p=P, k=TOPK)

    with ExitStack() as ctx:
        def sb(name, shape, dt=F32):
            return ctx.enter_context(nc.sbuf_tensor(name, shape, dt))

        def sem(name):
            return ctx.enter_context(nc.semaphore(name))

        bank = [ctx.enter_context(nc.psum_tensor(f"bank{i}", [P, 512], F32)) for i in range(8)]

        x_all = sb("x_all", [P, NT, D])
        xfT_all = sb("xfT_all", [P, N])
        gates = sb("gates", [P, NT, TOPK])
        cst = sb("cst", [P, const.shape[1]])

        def field(name):
            at, n = where[name]
            return cst[:, at:at + n]

        cos = field("cos").rearrange("p (t i) -> p t i", i=HALF)
        sin = field("sin").rearrange("p (t i) -> p t i", i=HALF)
        pen = field("pen")
        ident = field("ident")
        numbers = field("numbers")
        pair = field("pair").rearrange("p (t k) -> p t k", k=TOPK)

        wqkv = sb("wqkv", [P, 3 * D])
        wout = sb("wout", [P, D])
        ident_b = sb("ident_b", [P, P], BF16)
        before_b = sb("before_b", [P, P], BF16)
        ones_b = sb("ones_b", [P, P], BF16)
        maskq_b = sb("maskq_b", [P, P], BF16)
        comb_st = sb("comb_st", [P, H, P], BF16)
        comb_mv = sb("comb_mv", [P, 2, P], BF16)
        cent = sb("cent", [NGR + NE, D])
        cent_sq = sb("cent_sq", [NGR + NE, D])
        cent_n = sb("cent_n", [NGR + NE, 4])
        centT = sb("centT", [P, NGR + NE])
        bias_b = sb("bias_b", [P, NE])
        mhalf = sb("mhalf", [P, 4])
        st1 = sb("st1", [P, 6])
        st2 = sb("st2", [P, 6])
        mv1 = sb("mv1", [P, 2, 2])
        mv2 = sb("mv2", [P, 2, 2])
        pin = sb("pin", [P, 2, 3])
        pout = sb("pout", [P, 2, 3])
        ve = sb("ve", [P, 2])
        xn = sb("xn", [P, 2, D])
        xnT = sb("xnT", [P, 2, P])
        ra = sb("ra", [P, 2 * D])
        rb = sb("rb", [P, 2 * D])
        rr = sb("rr", [P, 2, 2 * D])
        r1 = sb("r1", [P, 2 * D])
        qk = sb("qk", [P, 2, 2, H, 8, DH], BF16)
        qT = sb("qT", [P, 2, NG, P], BF16)
        kT = sb("kT", [P, 2, NG, SPAN], BF16)
        v_cur = sb("v_cur", [P, 2, H, 32])
        v_mix = sb("v_mix", [P, 2, H, 32])
        mx = sb("mx", [P, 2, H])
        nm = sb("nm", [P, H])
        mp = sb("mp", [P, 2, 3, H], BF16)
        pt = sb("pt", [P, 2, NU, 512])
        pvT = sb("pvT", [P, 2, 512])
        rec = sb("rec", [P, H])
        on = sb("on", [P, 2, D])
        oT = sb("oT", [P, 2, P])
        xfe = sb("xfe", [P, 2, TOPK, ROW])
        xfT = sb("xfT", [P, 2, P])
        sc = sb("sc", [P, NGR + NE])
        es = sb("es", [P, NE])
        es2 = sb("es2", [P, NE])
        gm8 = sb("gm8", [P, 8])
        gi8 = sb("gi8", [P, 8], U32)
        geq = sb("geq", [P, NGR, TOPG])
        gsel = sb("gsel", [P, NGR])
        gpen = sb("gpen", [P, NGR])
        em8 = sb("em8", [P, 8])
        ei8 = sb("ei8", [P, 8], U32)
        ed4 = sb("ed4", [P, 2, TOPK])
        ex4 = sb("ex4", [P, 2, TOPK])
        exs = sb("exs", [P, 2, 1])
        exr = sb("exr", [P, 1])
        oh = sb("oh", [P, TOPK, NE])
        msel = sb("msel", [P, 2, NE], BF16)
        macc = sb("macc", [P, 2, NE], BF16)
        ohp = sb("ohp", [P, TOPK, NE])
        posk = sb("posk", [P, TOPK])
        keep = sb("keep", [P, TOPK])
        slotf = sb("slotf", [P, TOPK])
        slotf2 = sb("slotf2", [P, TOPK])
        sidx = sb("sidx", [P, 2, TOPK], U32)
        sgw = sb("sgw", [P, FF])
        suw = sb("suw", [P, FF])
        sdw = sb("sdw", [P, 2, D])
        wgu = sb("wgu", [P, 2, 2, FF])
        wdn = sb("wdn", [P, 2, 2, D])
        sact = sb("sact", [P, 2, 2, 512])
        fill = sb("fill", [P, ST, ROW])
        xg = sb("xg", [P, 2, ST, ROW])
        wgu_parts = sb("wgu_parts", [P, 2, 2, 2, FF], F32R)
        xgT_parts = sb("xgT_parts", [P, 2, 2, cap], F32R)
        hact = sb("hact", [P, 2, 2, cap])
        yout = sb("yout", [P, 2, ST, D])
        ypair = sb("ypair", [P, 2, ST])
        yidx = sb("yidx", [P, 2, ST], U32)
        rload = sb("rload", [P, NR, TOPK, D])
        gates_late = sb("gates_late", [P, NR, 2])

        names = """const_loaded x_first x_loaded wqkv_loaded attn_w_loaded w_loaded cent_loaded fill_done zero_done filled zeroed
        cent_sum cent_len cent_unit centT_done centT_evac casts comb_cast fills
        ln1 ln2 pow_done xn_ready xnT_done xnT_evac qkv_done rope_ab rope_r v_evac
        v_prev split_hi split_rest split_mid split_lo qkT_done qT_evac kT_evac k_prev p1_scores p1_reduced negm mT_done mT_evac
        p2_scores exp_done pv_done pv_evac pvT_done recip onorm oT_done oT_evac wout_done x1_ready xf_ready xf_copied xfe_id
        xfT_done xfT_evac xfT_kept router_done sc_ready route gate_exp gate_done sel_ready acc_ready pos_done
        pos_read slots slot_ready sh_gu sh_act sh_mul sh_down sh_added
        xgT_done xgT_hi xgT_lo wgu_hi wgu_lo gu_done h_act h_mul down_done y_evac
        ypair_ready yidx_ready late_gates late_gated late_sum comb_step stored""".split()
        S = namedtuple("Semaphores", names)(*[sem(n) for n in names])
        dispatched = [sem(f"dispatched{b}") for b in range(2)]
        wgu_arrived = [sem(f"wgu_arrived{b}") for b in range(2)]
        wdn_arrived = [sem(f"wdn_arrived{b}") for b in range(2)]
        xg_arrived = [sem(f"xg_arrived{b}") for b in range(2)]
        y_sent = [sem(f"y_sent{b}") for b in range(2)]
        r_arrived = [sem(f"r_arrived{b}") for b in range(NR // 2)]

        def wait(eng, s, value):
            if not (isinstance(value, int) and value < 1):
                eng.wait_ge(s, value)

        def hold(eng):
            eng.nop(nofuse=True)

        def attention_steps(eng, step):
            FIRST = 6
            LAST = FIRST + (NT - 1 - FIRST) // 2 * 2

            def straight(tau):
                step(tau, *[tile_of((tau - k) // 2, (tau - k) % 2) if 0 <= tau - k < NT else None
                            for k in range(-1, 5)])

            for tau in range(-1, FIRST):
                straight(tau)
            with eng.Fori(0, (LAST - FIRST) // 2) as i:
                for c in range(2):
                    step(2 * i + (FIRST + c), *[tile_of(i + (FIRST + c - k) // 2, (FIRST + c - k) % 2)
                                                for k in range(-1, 5)])
            for tau in range(LAST, NT + 4):
                straight(tau)

        def lagged_steps(eng, step, count, ahead):
            FIRST = 3
            LAST = FIRST + (count - 1 - FIRST) // 2 * 2
            lags = range(-1 if ahead else 0, 2)

            def straight(n):
                step(*[tile_of((n - k) // 2, (n - k) % 2) if 0 <= n - k < count else None for k in lags])

            for n in range(-1 if ahead else 0, FIRST):
                straight(n)
            with eng.Fori(0, (LAST - FIRST) // 2) as i:
                for c in range(2):
                    step(*[tile_of(i + (FIRST + c - k) // 2, (FIRST + c - k) % 2) for k in lags])
            for n in range(LAST, count + 1):
                straight(n)

        def shared_steps(step, start, end):
            for m in range(start, end + 1):
                step(tile_of(m // 2, m % 2) if m < end else None,
                     tile_of((m - 1) // 2, (m - 1) % 2) if m > start else None)

        block = ctx.enter_context(nc.Block())

        @block.sync
        def _(sp):
            sp.dma_start(cst[:, :], const).then_inc(S.const_loaded, 16)
            sp.dma_start(x_all[:, 0:4, :], x_v[:, 0:4, :]).then_inc(S.x_first, 16)
            sp.wait_ge(S.wqkv_loaded, 16)
            sp.dma_start(x_all[:, 4:NT, :], x_v[:, 4:NT, :]).then_inc(S.x_loaded, 16)
            sp.dma_start(sgw[:, :], s_g).then_inc(S.w_loaded, 16)
            sp.dma_start(suw[:, :], s_u).then_inc(S.w_loaded, 16)
            sp.dma_start(sdw[:, :, :], s_d.rearrange("(c p) n -> p c n", c=2)).then_inc(S.w_loaded, 16)

            def load_wgu(e, c):
                sp.dma_start(wgu[:, c, 0], w_g[e]).then_inc(wgu_arrived[c], 16)
                sp.dma_start(wgu[:, c, 1], w_u[e]).then_inc(wgu_arrived[c], 16)

            def load_wdn(e, c):
                sp.dma_start(wdn[:, c], w_d[e].rearrange("(h p) n -> p h n", p=P)).then_inc(wdn_arrived[c], 16)

            def load_slots(e, c):
                sp.dma_start(xg[:, c].rearrange("p j c -> p (j c)"), slots_v[e]).then_inc(xg_arrived[c], 16)

            sp.wait_ge(S.fill_done, 2)
            with sp.Fori(0, NE) as e:
                sp.dma_start(slots_v[e], fill[:, :, :].rearrange("p j c -> p (j c)")).then_inc(S.filled, 16)
            sp.wait_ge(S.zero_done, 1)
            with sp.Fori(0, NT) as t:
                sp.dma_start(pairs_v[t], rload[:, 0].rearrange("p k d -> p (k d)")).then_inc(S.zeroed, 16)

            for e in range(2):
                load_wgu(e, e)
                load_wdn(e, e)
            for b in range(2):
                sp.wait_ge(dispatched[b], 16 * TOPK * (NT // 2))
            for e in range(2):
                load_slots(e, e)
            def reload(e, c):
                sp.wait_ge(S.xgT_done, 2 * (e - 1))
                sp.wait_ge(S.ypair_ready, e - 1)
                load_slots(e, c)
                sp.wait_ge(S.wgu_lo, e - 1)
                load_wgu(e, c)

            def reload_down(e, c):
                sp.wait_ge(S.down_done, e - 1)
                load_wdn(e, c)

            reload(2, 0)
            with sp.Fori(0, (NE - 4) // 2) as i:
                for k in (3, 4):
                    reload(2 * i + k, k % 2)
                    reload_down(2 * i + (k - 1), (k - 1) % 2)
            reload(NE - 1, 1)
            reload_down(NE - 2, 0)
            reload_down(NE - 1, 1)

            for b in range(2):
                sp.wait_ge(y_sent[b], 16 * ST * (NE // 2))
            sp.wait_ge(S.zeroed, 16 * NT)
            pairs_in = pairs_d.rearrange("(t p k) d -> p t (k d)", p=P, k=TOPK)

            def load_results(q, c):
                sp.dma_start(rload[:, 2 * c:2 * c + 2].rearrange("p t k d -> p t (k d)"),
                             pairs_in[:, bass.ds(2 * q, 2), :]).then_inc(r_arrived[c], 16)

            for c in range(NR // 2):
                load_results(c, c)
            with sp.Fori(0, NT // NR - 1) as i:
                for c in range(NR // 2):
                    sp.wait_ge(S.comb_step, CSTEPS * ((NR // 2) * i + (c + 1)))
                    load_results((NR // 2) * i + (NR // 2 + c), c)

        @block.gpsimd
        def _(pool):
            g = nc.gpsimd
            g.memset(mhalf[:, :], -0.5).then_inc(S.cent_len, 1)
            g.memset(qk[:, :, :, :, :, :], 0.0).then_inc(S.fills, 1)
            g.memset(v_cur[:, :, :, :], 0.0).then_inc(S.fills, 1)
            g.memset(v_mix[:, :, :, :], 0.0).then_inc(S.fills, 1)
            pool.wait_ge(S.fills, 3)
            g.memset(qk[:, :, 0, :, 7, 0:1], 1.0).then_inc(S.fills, 1)
            g.memset(v_cur[:, :, :, DH:DH + 1], 1.0).then_inc(S.fills, 1)
            g.memset(v_mix[:, :, :, DH:DH + 1], 1.0).then_inc(S.fills, 1)
            g.memset(fill[:, :, 0:D], 0.0).then_inc(S.fill_done, 1)
            g.memset(fill[:, :, D:ROW], OOB).then_inc(S.fill_done, 1)
            g.memset(rload[:, 0], 0.0).then_inc(S.zero_done, 1)
            pool.wait_ge(S.cent_sum, 1)
            pool.wait_ge(S.cent_len, 1)
            g.tensor_scalar(cent_n[:, 1:2], cent_n[:, 0:1], 1e-24, None, ALU.max).then_inc(S.cent_len, 1)
            pool.wait_ge(S.cent_len, 2)
            g.tensor_tensor(cent_n[:, 2:3], cent_n[:, 1:2], mhalf[0:NGR + NE, 0:1], ALU.pow).then_inc(S.cent_len, 1)

            def step(tau, tn, tf, tp, ts, tw, tr):
                if tf is not None:
                    b = tf.b
                    pool.wait_ge(S.rope_ab, 3 * tf.n + 3)
                    wait(pool, S.split_hi, 2 * (tf.n - 1))
                    wait(pool, S.split_rest, tf.n - 1)
                    g.tensor_tensor(rr[:, b], ra[:, :], rb[:, :], ALU.add).then_inc(S.rope_r, 1)
                if tr is not None:
                    pool.wait_ge(S.xfT_evac, tr.n + 1)
                    hold(pool)
                    g.tensor_copy(xfT_all[:, bass.ts(tr.n, P)], xfT[:, tr.b]).then_inc(S.xfT_kept, 1)
                if tw is not None or tn is not None:
                    lo, hi = (0 if tn is not None else 1), (3 if tw is not None else 1)
                    c = tn.b if tn is not None else tw.b
                    if tn is not None:
                        pool.wait_ge(S.ln1, 3 * tn.n + 3)
                    if tw is not None:
                        pool.wait_ge(S.ln2, 6 * tw.n + 6)
                    if isinstance(tau, int) and tau == -1:
                        pool.wait_ge(S.cent_len, 1)
                    g.tensor_tensor(pout[:, c, lo:hi], pin[:, c, lo:hi], mhalf[:, lo:hi], ALU.pow)\
                     .then_inc(S.pow_done, 1)
                if tf is not None:
                    pool.wait_ge(S.split_mid, 2 * tf.n + 2)
                    r = r1[:, :].rearrange("p (w h d) -> p w h d", w=2, h=H)
                    g.tensor_tensor(qk[:, tf.b, 0, :, 2, :], r[:, 0], qk[:, tf.b, 0, :, 4, :], ALU.subtract)\
                     .then_inc(S.split_lo, 1)
                    g.tensor_tensor(qk[:, tf.b, 1, :, 6, :], r[:, 1], qk[:, tf.b, 1, :, 4, :], ALU.subtract)\
                     .then_inc(S.split_lo, 1)
                if tw is not None:
                    wait(pool, dispatched[tw.b], 16 * TOPK * tw.half)
                    hold(pool)
                    g.tensor_copy(xfe[:, tw.b, :, D:ROW], pair[:, bass.ds(tw.n, 1), :].rearrange("p o k -> p k o"))\
                     .then_inc(S.xfe_id, 1)
                if tr is not None:
                    if isinstance(tr.n, int) and tr.n == 0:
                        pool.wait_ge(S.filled, 16 * NE)
                    pool.wait_ge(S.slot_ready, tr.n + 1)
                    pool.wait_ge(S.xfe_id, tr.n + 1)
                    pool.wait_ge(S.xf_ready, tr.n + 1)
                    pool.wait_ge(S.xf_copied, tr.n + 1)
                    hold(pool)
                    for k in range(TOPK):
                        g.indirect_dma_start(
                            out=slots_d, out_offset=bass.IndirectOffsetOnAxis(ap=sidx[:, tr.b, k:k + 1], axis=0),
                            in_=xfe[:, tr.b, k, :], in_offset=None, bounds_check=NSLOT - 1,
                            oob_is_err=False).then_inc(dispatched[tr.b], 16)

            attention_steps(pool, step)

            pool.wait_ge(S.zeroed, 16 * NT)
            with pool.Fori(0, NE // 2) as i:
                for c in range(2):
                    e = 2 * i + c
                    pool.wait_ge(S.yidx_ready, e + 1)
                    pool.wait_ge(S.y_evac, 2 * e + 2)
                    hold(pool)
                    for j in range(ST):
                        g.indirect_dma_start(
                            out=pairs_d, out_offset=bass.IndirectOffsetOnAxis(ap=yidx[:, c, j:j + 1], axis=0),
                            in_=yout[:, c, j, :], in_offset=None, bounds_check=N * TOPK - 1,
                            oob_is_err=False).then_inc(y_sent[c], 16)

            pool.wait_ge(S.gate_done, 2 * NT)
            with pool.Fori(0, NT // NR) as i:
                for c in range(NR // 2):
                    q = (NR // 2) * i + c
                    tiles = slice(2 * c, 2 * c + 2)
                    g.tensor_copy(gates_late[:, tiles, :], gates[:, bass.ds(2 * q, 2), 2:TOPK])\
                     .then_inc(S.late_gates, 1)
                    pool.wait_ge(r_arrived[c], 16 * (i + 1))
                    pool.wait_ge(S.late_gates, q + 1)
                    hold(pool)
                    g.tensor_tensor(rload[:, tiles, 2:TOPK, :], rload[:, tiles, 2:TOPK, :],
                                    gates_late[:, tiles, :].unsqueeze(3).broadcast_to([P, 2, 2, D]), ALU.mult)\
                     .then_inc(S.late_gated, 1)
                    pool.wait_ge(S.late_gated, q + 1)
                    g.tensor_tensor(rload[:, tiles, 2, :], rload[:, tiles, 2, :], rload[:, tiles, 3, :], ALU.add)\
                     .then_inc(S.late_sum, 1)

        @block.scalar
        def _(act):
            a = nc.scalar
            act.dma_start(cent[0:NGR, :], group_c).then_inc(S.cent_loaded, 16)
            act.dma_start(cent[NGR:NGR + NE, :], expert_c).then_inc(S.cent_loaded, 16)
            act.dma_start(wqkv[:, :], w_qkv).then_inc(S.wqkv_loaded, 16)
            act.dma_start(wout[:, :], w_out).then_inc(S.attn_w_loaded, 16)
            act.dma_start(bias_b[:, :], bias.rearrange("(o e) -> o e", o=1).broadcast_to([P, NE]))\
               .then_inc(S.attn_w_loaded, 16)
            act.wait_ge(S.cent_loaded, 32)
            a.activation(cent_sq[:, :], cent[:, :], ACT.Square, accum_out=cent_n[:, 0:1]).then_inc(S.cent_sum, 1)
            act.wait_ge(S.const_loaded, 16)
            a.copy(comb_st[0:WIN], field("comb")[0:WIN].unsqueeze(1).broadcast_to([WIN, H, P])).then_inc(S.comb_cast, 1)
            a.copy(comb_st[WIN:WIN + 3 * H], field("head_rows")[WIN:WIN + 3 * H].unsqueeze(2)
                   .broadcast_to([3 * H, H, P])).then_inc(S.comb_cast, 1)

            def step(tau, tn, tf, tp, ts, tw, tr):
                def high_parts(w):
                    if tf is not None:
                        act.wait_ge(S.rope_r, tf.n + 1)
                        if isinstance(tf.n, int) and tf.n == 0:
                            act.wait_ge(S.fills, 6)
                        wait(act, S.qkT_done, 2 * (tf.n - 1))
                        wait(act, S.split_lo, 2 * (tf.n - 1))
                        a.copy(qk[:, tf.b, w, :, (Q_HI, K_HI)[w], :],
                               rr[:, tf.b, w * D:(w + 1) * D].rearrange("p (h d) -> p h d", h=H)
                               .unsqueeze(2).broadcast_to([P, H, 3, DH])).then_inc(S.split_hi, 1)

                def exponentials(u):
                    if ts is not None:
                        wait(act, S.pv_done, ts.n - 1)
                        act.wait_ge(S.p2_scores, NU * ts.n + (u + 1))
                        a.activation(pt[:, ts.b, u], bank[2 + u % 2][:, :], ACT.Exp, scale=QK_SCALE)\
                         .then_inc(S.exp_done, 1)
                if tr is not None:
                    act.wait_ge(S.xfT_done, tr.n + 1)
                    wait(act, S.router_done, tr.n - 1)
                    wait(act, S.xfT_kept, tr.n - 1)
                    a.copy(xfT[:, tr.b], bank[4][:, 3 * D:3 * D + P]).then_inc(S.xfT_evac, 1)
                if tf is not None:
                    act.wait_ge(S.xnT_done, tf.n + 1)
                    wait(act, S.qkv_done, tf.n - 1)
                    a.copy(xnT[:, tf.b], bank[3][:, 2 * P:3 * P]).then_inc(S.xnT_evac, 1)
                if tp is not None:
                    act.wait_ge(S.qkT_done, 2 * tp.n + 2)
                    wait(act, S.k_prev, tp.n - 1)
                    wait(act, S.p2_scores, NU * (tp.n - 1))
                    a.copy(kT[:, tp.b, :, WIN:SPAN], bank[6][:, :].bitcast(BF16).rearrange("p (g t) -> p g t", g=NG))\
                     .then_inc(S.kT_evac, 1)
                if tr is not None:
                    act.wait_ge(S.xf_ready, tr.n + 1)
                    a.copy(xfe[:, tr.b, 1:TOPK, 0:D], xfe[:, tr.b, 0:1, 0:D].broadcast_to([P, TOPK - 1, D]))\
                     .then_inc(S.xf_copied, 1)
                if tw is not None:
                    act.wait_ge(S.oT_done, tw.n + 1)
                    wait(act, S.wout_done, tw.n - 1)
                    a.copy(oT[:, tw.b], bank[3][:, 0:P]).then_inc(S.oT_evac, 1)
                exponentials(0)
                high_parts(0)
                high_parts(1)
                exponentials(1)
                if tr is not None:
                    act.wait_ge(S.route, 12 * tr.n + 10)
                    wait(act, S.gate_done, 2 * (tr.n - 1))
                    a.activation(ex4[:, tr.b], ed4[:, tr.b], ACT.Exp, accum_out=exs[:, tr.b]).then_inc(S.gate_exp, 1)
                exponentials(2)
                exponentials(3)
                if ts is not None:
                    act.wait_ge(S.pv_done, ts.n + 1)
                    wait(act, S.pvT_done, ts.n - 1)
                    a.copy(pvT[:, ts.b], bank[7][:, :]).then_inc(S.pv_evac, 1)
                if tf is not None:
                    b = tf.b
                    v = bank[4][:, 2 * D:3 * D].rearrange("p (h d) -> p h d", h=H)
                    act.wait_ge(S.rope_ab, 3 * tf.n + 3)
                    wait(act, S.pv_done, tf.n - 1)
                    wait(act, S.v_prev, tf.n - 1)
                    a.copy(v_cur[:, b, :, 0:DH], v).then_inc(S.v_evac, 1)
                    a.copy(v_mix[WIN:P, b, :, 0:DH], v[0:WIN]).then_inc(S.v_evac, 1)
                    if not isinstance(tf.n, int) or tf.n:
                        act.wait_ge(S.v_evac, 2 * tf.n)
                        a.copy(v_mix[0:WIN, b, :, 0:DH], v_cur[WIN:P, 1 - b, :, 0:DH]).then_inc(S.v_prev, 1)
                if tp is not None:
                    act.wait_ge(S.mT_done, tp.n + 1)
                    wait(act, S.p2_scores, NU * (tp.n - 1))
                    a.copy(comb_mv[WIN:WIN + 3 * H, tp.b, :], bank[1][:, :].bitcast(BF16)[0:3 * H, 0:P])\
                     .then_inc(S.mT_evac, 1)
                if tf is not None:
                    wait(act, S.p2_scores, NU * (tf.n - 1))
                    act.wait_ge(S.qkT_done, 2 * tf.n + 1)
                    a.copy(qT[:, tf.b], bank[5][:, :].bitcast(BF16).rearrange("p (g t) -> p g t", g=NG))\
                     .then_inc(S.qT_evac, 1)

            attention_steps(act, step)

            def shared_step(m, _):
                if m is not None:
                    for h in range(2):
                        act.wait_ge(S.sh_gu, 4 * m.n + (2 * h + 1))
                        wait(act, S.sh_down, m.n - 1)
                        a.activation(sact[:, m.b, h], bank[h][:, :], ACT.Silu).then_inc(S.sh_act, 1)

            shared_steps(shared_step, 0, SHARED_EARLY)

            def expert_step(en, e, ed):
                def silu(ch):
                    for h in range(2):
                        act.wait_ge(S.gu_done, 8 * e.n + (4 * ch + 2 * h + 1))
                        a.activation(hact[:, e.b, h, ch * CH:(ch + 1) * CH], bank[2 + h][:, 0:CH], ACT.Silu)\
                         .then_inc(S.h_act, 1)

                if en is not None:
                    act.wait_ge(wgu_arrived[en.b], 32 * (en.half + 1))
                    wait(act, S.gu_done, 8 * (en.n - 1))
                    a.copy(wgu_parts[:, en.b, 0], wgu[:, en.b]).then_inc(S.wgu_hi, 1)
                if e is not None:
                    wait(act, S.down_done, e.n - 1)
                    silu(0)
                if ed is not None:
                    act.wait_ge(S.down_done, ed.n + 1)
                    wait(act, y_sent[ed.b], 16 * ST * ed.half)
                    a.copy(yout[:, ed.b, 0:4], bank[6][:, :].rearrange("p (j d) -> p j d", d=D))\
                     .then_inc(S.y_evac, 1)
                    a.copy(yout[:, ed.b, 4:ST], bank[7][:, 0:D].rearrange("p (j d) -> p j d", d=D))\
                     .then_inc(S.y_evac, 1)
                if e is not None:
                    silu(1)

            lagged_steps(act, expert_step, NE, True)
            shared_steps(shared_step, SHARED_EARLY, N // 512)

            with act.Fori(0, NT // 2) as i:
                act.wait_ge(S.comb_step, CSTEPS * (i + 1))
                act.dma_start(out_v[:, bass.ds(2 * i, 2), :], x_all[:, bass.ds(2 * i, 2), :]).then_inc(S.stored, 16)
            act.wait_ge(S.stored, 16 * NT // 2)

        @block.tensor
        def _(pe):
            mm = nc.tensor.matmul
            pe.wait_ge(S.casts, 7)
            pe.wait_ge(S.wqkv_loaded, 16)
            pe.wait_ge(S.attn_w_loaded, 16 * 2)

            def step(tau, tn, tf, tp, ts, tw, tr):
                def first_scores(u):
                    s, g4 = u % NS, u // NS * 4
                    bk = bank[u % 2]
                    wait(pe, S.p1_reduced, NU * tp.n + (u - 1) if not isinstance(tp.n, int) or tp.n else u - 1)
                    if u == 1:
                        wait(pe, S.mT_evac, tp.n)
                    mm(bk[:, :].rearrange("p (c j) -> p c j", c=4), ident_b[:, :],
                       maskq_b[:, :].unsqueeze(1).broadcast_to([P, 4, P]), start=True, stop=False,
                       skip_group_check=True)
                    rows = slice(STRIP * s, STRIP * (s + 1))
                    for hb in range(2):
                        for c in range(4):
                            last = mm(bk[hb * WIN:(hb + 1) * WIN, c * P:(c + 1) * P],
                                      qT[rows, tp.b, g4 + c, hb * WIN:(hb + 1) * WIN],
                                      kT[rows, tp.b, g4 + c, hb * WIN:hb * WIN + P], start=False, stop=(c == 3),
                                      skip_group_check=True)
                    last.then_inc(S.p1_scores, 1)

                def second_scores(u):
                    s, g4 = u % NS, u // NS * 4
                    bk = bank[2 + u % 2]
                    wait(pe, S.exp_done, NU * ts.n + (u - 1) if not isinstance(ts.n, int) or ts.n else u - 1)
                    for c in range(4):
                        mm(bk[:, c * P:(c + 1) * P], comb_st[0:WIN + 3 * H, NS * (g4 + c) + s, :],
                           comb_mv[0:WIN + 3 * H, ts.b, :], start=(c == 0), stop=False, skip_group_check=True)
                    rows = slice(STRIP * s, STRIP * (s + 1))
                    for c in range(4):
                        for hb in range(2):
                            at = c * P + hb * WIN
                            last = mm(bk[:, at:at + WIN], kT[rows, ts.b, g4 + c, hb * WIN:hb * WIN + P],
                                      qT[rows, ts.b, g4 + c, hb * WIN:(hb + 1) * WIN], start=False,
                                      stop=(c == 3 and hb == 1), skip_group_check=True)
                    last.then_inc(S.p2_scores, 1)

                def weighted_values(u):
                    pe.wait_ge(S.exp_done, NU * ts.n + (u + 1))
                    for c in range(4):
                        h = NS * (u // NS * 4 + c) + u % NS
                        for hb in range(2):
                            vals = (v_cur if hb else v_mix)[:, ts.b, h, :]
                            at = c * P + hb * WIN
                            to = h // 4 * P + hb * WIN
                            last = mm(bank[7][32 * (h % 4):32 * (h % 4 + 1), to:to + WIN], vals,
                                      pt[:, ts.b, u, at:at + WIN], start=True, stop=True)
                    return last

                def transposed_parts(t, w):
                    pe.wait_ge(S.split_hi, 2 * t.n + 2)
                    pe.wait_ge(S.split_lo, 2 * t.n + 2)
                    wait(pe, (S.qT_evac, S.kT_evac)[w], t.n)
                    for gg in range(NG):
                        last = nc.tensor.transpose(
                            bank[5 + w][:, :].bitcast(BF16)[:, gg * P:(gg + 1) * P],
                            qk[:, t.b, w, NS * gg:NS * (gg + 1)].rearrange("p h c d -> p (h c d)"),
                            ident_b[:, :])
                    last.then_inc(S.qkT_done, 1)
                if tr is not None:
                    pe.wait_ge(S.xf_ready, tr.n + 1)
                    pe.wait_ge(S.v_evac, min(2 * (tr.n + 4), 2 * NT) if isinstance(tr.n, int) else 2 * (tr.n + 4))
                    nc.tensor.transpose(bank[4][:, 3 * D:3 * D + P], xfe[:, tr.b, 0, 0:D], ident[:, :])\
                      .then_inc(S.xfT_done, 1)
                if tf is not None:
                    pe.wait_ge(S.xn_ready, tf.n + 1)
                    wait(pe, S.exp_done, NU * (tf.n - 2))
                    nc.tensor.transpose(bank[3][:, 2 * P:3 * P], xn[:, tf.b], ident[:, :]).then_inc(S.xnT_done, 1)
                if tp is not None:
                    wait(pe, S.pos_read, tp.n - 3)
                    transposed_parts(tp, 1)
                if tr is not None:
                    pe.wait_ge(S.xfT_evac, tr.n + 1)
                    pe.wait_ge(S.pv_evac, min(tr.n + 2, NT) if isinstance(tr.n, int) else tr.n + 2)
                    mm(bank[7][:, 0:NGR + NE], xfT[:, tr.b], centT[:, :], start=True, stop=True)\
                      .then_inc(S.router_done, 1)
                if tf is not None:
                    pe.wait_ge(S.xnT_evac, tf.n + 1)
                    wait(pe, S.v_evac, 2 * tf.n)
                    if tr is not None:
                        pe.wait_ge(S.xfT_evac, tr.n + 1)
                    mm(bank[4][:, 0:3 * D], xnT[:, tf.b], wqkv[:, :], start=True, stop=True).then_inc(S.qkv_done, 1)
                    if isinstance(tf.n, int) and tf.n == 0:
                        pe.wait_ge(S.cent_unit, 1)
                        nc.tensor.transpose(bank[0][:, 0:NGR + NE], cent_sq[:, :], ident[0:NGR + NE, 0:NGR + NE])\
                          .then_inc(S.centT_done, 1)
                        pe.wait_ge(S.fills, 6)
                        pe.wait_ge(S.comb_cast, 2)
                        pe.wait_ge(S.centT_evac, 1)
                if tw is not None:
                    pe.wait_ge(S.onorm, tw.n + 1)
                    if tf is not None:
                        pe.wait_ge(S.xnT_evac, tf.n + 1)
                    nc.tensor.transpose(bank[3][:, 0:P], on[:, tw.b], ident[:, :]).then_inc(S.oT_done, 1)
                if tp is not None:
                    pe.wait_ge(S.qT_evac, tp.n + 1)
                    pe.wait_ge(S.kT_evac, tp.n + 1)
                    wait(pe, S.k_prev, tp.n)
                    first_scores(0)
                if tw is not None:
                    pe.wait_ge(S.oT_evac, tw.n + 1)
                    mm(bank[3][:, P:2 * P], oT[:, tw.b], wout[:, :], start=True, stop=True).then_inc(S.wout_done, 1)
                if tp is not None:
                    first_scores(1)
                if ts is not None:
                    pe.wait_ge(S.mT_evac, ts.n + 1)
                    wait(pe, S.onorm, ts.n)
                    second_scores(0)
                if tp is not None:
                    first_scores(2)
                if tp is not None:
                    first_scores(3)
                if ts is not None:
                    wait(pe, S.x1_ready, ts.n)
                    if tf is not None:
                        pe.wait_ge(S.xnT_evac, tf.n + 1)
                    second_scores(1)
                if ts is not None:
                    second_scores(2)
                if ts is not None:
                    pe.wait_ge(S.v_evac, 2 * ts.n + 2)
                    wait(pe, S.v_prev, ts.n)
                    wait(pe, S.pv_evac, ts.n)
                    if tr is not None:
                        pe.wait_ge(S.sc_ready, tr.n + 1)
                    weighted_values(0)
                if ts is not None:
                    second_scores(3)
                if tr is not None:
                    pe.wait_ge(S.sel_ready, tr.n + 1)
                    wait(pe, S.acc_ready, tr.n)
                    pe.wait_ge(S.kT_evac, min(tr.n + 4, NT) if isinstance(tr.n, int) else tr.n + 4)
                    wait(pe, S.pos_read, tr.n)
                    mm(bank[6][:, P:P + NE], before_b[:, :], msel[:, tr.b], start=True, stop=False)
                    mm(bank[6][:, P:P + NE], ones_b[:, :], macc[:, tr.b], start=False, stop=True)\
                      .then_inc(S.pos_done, 1)
                if ts is not None:
                    weighted_values(1)
                if ts is not None:
                    weighted_values(2)
                if ts is not None:
                    weighted_values(3).then_inc(S.pv_done, 1)
                if tp is not None:
                    pe.wait_ge(S.p1_reduced, NU * tp.n + NU)
                    pe.wait_ge(S.negm, 4 * tp.n + 4)
                    hold(pe)
                    nc.tensor.transpose(bank[1][:, :].bitcast(BF16)[0:3 * H, 0:P],
                                        mp[:, tp.b].rearrange("p c h -> p (c h)"), ident_b[:, :])\
                      .then_inc(S.mT_done, 1)
                if tf is not None:
                    transposed_parts(tf, 0)
                if ts is not None:
                    pe.wait_ge(S.pv_evac, ts.n + 1)
                    pe.wait_ge(S.exp_done, NU * ts.n + NU)
                    for q in range(4):
                        last = nc.tensor.transpose(bank[2][:, q * P:(q + 1) * P], pvT[:, ts.b, q * P:(q + 1) * P],
                                                   ident[:, :])
                    last.then_inc(S.pvT_done, 1)

            attention_steps(pe, step)

            pe.wait_ge(S.w_loaded, 16 * 3)
            pe.wait_ge(S.mT_evac, NT)
            pe.wait_ge(S.v_evac, 2 * NT)
            pe.wait_ge(S.pos_read, NT)
            pe.wait_ge(S.xfT_kept, NT)
            pe.wait_ge(S.x1_ready, NT)

            def shared_step(m, md):
                if m is not None:
                    for h in range(2):
                        cols = slice(h * P, (h + 1) * P)
                        wait(pe, S.sh_act, 2 * m.n + (h - 1) if not isinstance(m.n, int) or m.n else 0)
                        mm(bank[h][:, :], sgw[:, cols], xfT_all[:, bass.ts(m.n, 512)], start=True, stop=True)\
                          .then_inc(S.sh_gu, 1)
                        wait(pe, S.sh_mul, 2 * m.n + (h - 1) if not isinstance(m.n, int) or m.n else 0)
                        mm(bank[2 + h][:, :], suw[:, cols], xfT_all[:, bass.ts(m.n, 512)], start=True, stop=True)\
                          .then_inc(S.sh_gu, 1)
                if md is not None:
                    pe.wait_ge(S.sh_mul, 2 * md.n + 2)
                    wait(pe, S.sh_added, md.n - 1)
                    for j in range(4):
                        for h in range(2):
                            last = mm(bank[4 + md.b][:, j * D:(j + 1) * D], sact[:, md.b, h, j * P:(j + 1) * P],
                                      sdw[:, h, :], start=(h == 0), stop=(h == 1))
                    last.then_inc(S.sh_down, 1)

            shared_steps(shared_step, 0, SHARED_EARLY)
            pe.wait_ge(S.sh_added, SHARED_EARLY)

            def expert_step(en, e, ed):
                def gate_up(ch):
                    for h in range(2):
                        for w in range(2):
                            wait(pe, (S.h_act, S.h_mul)[w],
                                 4 * e.n + (2 * ch + h - 1) if not isinstance(e.n, int) or e.n else 2 * ch + h - 1)
                            for wp, xp in ((0, 0), (0, 1), (1, 0)):
                                last = mm(bank[2 + 2 * w + h][:, 0:CH],
                                          wgu_parts[:, e.b, wp, w, h * P:(h + 1) * P],
                                          xgT_parts[:, e.b, xp, ch * CH:(ch + 1) * CH],
                                          start=(wp + xp == 0), stop=(wp == 1))
                            last.then_inc(S.gu_done, 1)

                if en is not None:
                    pe.wait_ge(xg_arrived[en.b], 16 * (en.half + 1))
                    wait(pe, S.xgT_lo, 2 * en.n)
                    for j in range(ST):
                        tt = nc.tensor.transpose(bank[j // 4][:, j % 4 * P:(j % 4 + 1) * P], xg[:, en.b, j, 0:D],
                                                 ident[:, :])
                        if j == 3 or j == ST - 1:
                            tt.then_inc(S.xgT_done, 1)
                if e is not None:
                    pe.wait_ge(S.wgu_hi, e.n + 1)
                    pe.wait_ge(S.wgu_lo, e.n + 1)
                    pe.wait_ge(S.xgT_lo, 2 * e.n + 2)
                    gate_up(0)
                if ed is not None:
                    pe.wait_ge(wdn_arrived[ed.b], 16 * (ed.half + 1))
                    pe.wait_ge(S.h_mul, 4 * ed.n + 4)
                    wait(pe, S.y_evac, 2 * ed.n)
                    for j in range(ST):
                        for h in range(2):
                            last = mm(bank[6 + j // 4][:, j % 4 * D:(j % 4 + 1) * D],
                                      hact[:, ed.b, h, j * P:(j + 1) * P], wdn[:, ed.b, h, :],
                                      start=(h == 0), stop=(h == 1))
                    last.then_inc(S.down_done, 1)
                if e is not None:
                    gate_up(1)

            lagged_steps(pe, expert_step, NE, True)
            pe.wait_ge(S.h_act, 4 * NE)
            pe.wait_ge(S.h_mul, 4 * NE)
            shared_steps(shared_step, SHARED_EARLY, N // 512)

        @block.vector
        def _(dve):
            v = nc.vector
            v.memset(ones_b[:, :], 1.0).then_inc(S.casts, 1)
            v.memset(macc[:, 0], 0.0).then_inc(S.casts, 1)
            dve.wait_ge(S.const_loaded, 16)
            casts = [
                v.tensor_copy(ident_b[:, :], ident),
                v.tensor_copy(before_b[:, :], field("before")),
                v.tensor_copy(maskq_b[:, :], field("maskq")),
                v.tensor_copy(comb_mv[0:WIN], field("eye2")[0:WIN].unsqueeze(1).broadcast_to([WIN, 2, P])),
                v.tensor_copy(kT[:, 0, :, 0:WIN], pen[:, 0:1].unsqueeze(2).broadcast_to([P, NG, WIN])),
            ]
            for ins in casts:
                ins.then_inc(S.casts, 1)
            dve.wait_ge(S.x_first, 16)

            def step(tau, tn, tf, tp, ts, tw, tr):
                def maxima(u):
                    m = mx[:, tp.b].rearrange("p (g s) -> p g s", s=NS)
                    s, g4 = u % NS, u // NS * 4
                    dve.wait_ge(S.p1_scores, NU * tp.n + (u + 1))
                    v.tensor_reduce(m[:, g4:g4 + 4, s], bank[u % 2][:, :].rearrange("p (c j) -> p c j", c=4),
                                    AX.X, ALU.max).then_inc(S.p1_reduced, 1)

                R = 12
                by_group = lambda ap: ap.rearrange("p (g e) -> p g e", g=NGR)
                row = lambda t: x_all[:, bass.ds(t.n, 1), :].rearrange("p o d -> p (o d)")
                pv = bank[2][:, :].rearrange("p (h d) -> p h d", h=H)

                def weight_sums():
                    dve.wait_ge(S.pvT_done, tw.n + 1)
                    wait(dve, S.onorm, tw.n)
                    v.reciprocal(rec[:, :], pv[:, :, DH]).then_inc(S.recip, 1)

                def over_sums():
                    dve.wait_ge(S.recip, tw.n + 1)
                    wait(dve, S.oT_done, tw.n - 1)
                    v.tensor_tensor(on[:, tw.b].rearrange("p (h d) -> p h d", h=H), pv[:, :, 0:DH],
                                    rec[:, :].unsqueeze(2).broadcast_to([P, H, DH]), ALU.mult).then_inc(S.onorm, 1)

                def add_attention():
                    dve.wait_ge(S.wout_done, tw.n + 1)
                    v.tensor_tensor(row(tw), row(tw), bank[3][:, P:2 * P], ALU.add).then_inc(S.x1_ready, 1)

                def second_stats():
                    dve.wait_ge(S.x1_ready, tw.n + 1)
                    hold(dve)
                    v.bn_stats(st2[:, :], row(tw)).then_inc(S.ln2, 1)

                def second_mean():
                    dve.wait_ge(S.ln2, 6 * tw.n + 1)
                    hold(dve)
                    v.bn_aggr(mv2[:, tw.b], st2[:, :]).then_inc(S.ln2, 1)

                def second_var():
                    dve.wait_ge(S.ln2, 6 * tw.n + 2)
                    v.tensor_scalar(pin[:, tw.b, 1:2], mv2[:, tw.b, 1:2], EPS, None, ALU.add).then_inc(S.ln2, 1)

                def length_a():
                    dve.wait_ge(S.ln2, 6 * tw.n + 3)
                    v.reciprocal(ve[:, 0:1], pin[:, tw.b, 1:2]).then_inc(S.ln2, 1)

                def length_b():
                    dve.wait_ge(S.ln2, 6 * tw.n + 4)
                    v.tensor_scalar(ve[:, 1:2], ve[:, 0:1], mv2[:, tw.b, 1:2], float(D), ALU.mult, ALU.mult)\
                     .then_inc(S.ln2, 1)

                def length_c():
                    dve.wait_ge(S.ln2, 6 * tw.n + 5)
                    v.tensor_scalar(pin[:, tw.b, 2:3], ve[:, 1:2], 1e-24, None, ALU.max).then_inc(S.ln2, 1)

                def second_norm():
                    dve.wait_ge(S.pow_done, tau + 2)
                    wait(dve, dispatched[tw.b], 16 * TOPK * tw.half)
                    wait(dve, S.xfT_done, tw.n - 1)
                    v.tensor_scalar(xfe[:, tw.b, 0, 0:D], row(tw),
                                    mv2[:, tw.b, 0:1], pout[:, tw.b, 1:2], ALU.subtract, ALU.mult)\
                     .then_inc(S.xf_ready, 1)

                def first_stats():
                    if isinstance(tn.n, int) and tn.n == 4:
                        dve.wait_ge(S.x_loaded, 16)
                    v.bn_stats(st1[:, :], row(tn)).then_inc(S.ln1, 1)

                def first_mean():
                    dve.wait_ge(S.ln1, 3 * tn.n + 1)
                    hold(dve)
                    v.bn_aggr(mv1[:, tn.b], st1[:, :]).then_inc(S.ln1, 1)

                def first_var():
                    dve.wait_ge(S.ln1, 3 * tn.n + 2)
                    v.tensor_scalar(pin[:, tn.b, 0:1], mv1[:, tn.b, 1:2], EPS, None, ALU.add).then_inc(S.ln1, 1)

                def first_norm():
                    dve.wait_ge(S.pow_done, tau + 2)
                    wait(dve, S.xnT_done, tn.n - 1)
                    v.tensor_scalar(xn[:, tn.b], row(tn), mv1[:, tn.b, 0:1], pout[:, tn.b, 0:1], ALU.subtract,
                                    ALU.mult).then_inc(S.xn_ready, 1)

                def rotate(part):
                    z = bank[4][:, 0:2 * D].rearrange("p (h c i) -> p h c i", c=2, i=HALF)
                    zb = rb[:, :].rearrange("p (h c i) -> p h c i", c=2, i=HALF)
                    ct = cos[:, bass.ds(tf.n, 1), :].broadcast_to([P, 4 * H, HALF])
                    stn = sin[:, bass.ds(tf.n, 1), :].broadcast_to([P, 2 * H, HALF])
                    if part == 0:
                        dve.wait_ge(S.qkv_done, tf.n + 1)
                        wait(dve, S.rope_r, tf.n)
                        v.tensor_tensor(ra[:, :].rearrange("p (m i) -> p m i", i=HALF),
                                        bank[4][:, 0:2 * D].rearrange("p (m i) -> p m i", i=HALF), ct,
                                        ALU.mult).then_inc(S.rope_ab, 1)
                    elif part == 1:
                        v.scalar_tensor_tensor(zb[:, :, 0], z[:, :, 1], -1.0, stn, ALU.mult, ALU.mult)\
                         .then_inc(S.rope_ab, 1)
                    else:
                        v.tensor_tensor(zb[:, :, 1], z[:, :, 0], stn, ALU.mult).then_inc(S.rope_ab, 1)

                def rest():
                    dve.wait_ge(S.split_hi, 2 * tf.n + 2)
                    wait(dve, S.split_lo, 2 * tf.n)
                    v.tensor_tensor(r1[:, :].rearrange("p (m d) -> p m d", d=DH),
                                    rr[:, tf.b].rearrange("p (m d) -> p m d", d=DH),
                                    qk[:, tf.b, :, :, 0, :].rearrange("p w h d -> p (w h) d"), ALU.subtract)\
                     .then_inc(S.split_rest, 1)

                def middle(w):
                    dve.wait_ge(S.split_rest, tf.n + 1)
                    src = r1[:, w * D:(w + 1) * D].rearrange("p (h d) -> p h d", h=H)
                    v.tensor_copy(qk[:, tf.b, w, :, (Q_MID, K_MID)[w], :],
                                  src.unsqueeze(2).broadcast_to([P, H, 2, DH])).then_inc(S.split_mid, 1)

                def earlier_keys():
                    if not isinstance(tp.n, int) or tp.n:
                        dve.wait_ge(S.kT_evac, tp.n)
                        wait(dve, S.p2_scores, NU * (tp.n - 1))
                        v.tensor_scalar(kT[:, tp.b, :, 0:WIN], kT[:, 1 - tp.b, :, P:SPAN],
                                        pen[:, bass.ds(tp.n, 1)], None, ALU.add).then_inc(S.k_prev, 1)

                def maxima(u):
                    m = mx[:, tp.b].rearrange("p (g s) -> p g s", s=NS)
                    s, g4 = u % NS, u // NS * 4
                    dve.wait_ge(S.p1_scores, NU * tp.n + (u + 1))
                    v.tensor_reduce(m[:, g4:g4 + 4, s], bank[u % 2][:, :].rearrange("p (c j) -> p c j", c=4),
                                    AX.X, ALU.max).then_inc(S.p1_reduced, 1)

                def minus_hi():
                    dve.wait_ge(S.p1_reduced, NU * tp.n + NU)
                    wait(dve, S.mT_done, tp.n - 1)
                    v.tensor_scalar(mp[:, tp.b, 0], mx[:, tp.b], -1.0, None, ALU.mult).then_inc(S.negm, 1)

                def minus_rest():
                    dve.wait_ge(S.negm, 4 * tp.n + 1)
                    v.scalar_tensor_tensor(nm[:, :], mx[:, tp.b], -1.0, mp[:, tp.b, 0], ALU.mult,
                                           ALU.subtract).then_inc(S.negm, 1)

                def minus_mid():
                    dve.wait_ge(S.negm, 4 * tp.n + 2)
                    v.tensor_copy(mp[:, tp.b, 1], nm[:, :]).then_inc(S.negm, 1)

                def minus_lo():
                    dve.wait_ge(S.negm, 4 * tp.n + 3)
                    v.tensor_tensor(mp[:, tp.b, 2], nm[:, :], mp[:, tp.b, 1], ALU.subtract).then_inc(S.negm, 1)

                def scores():
                    dve.wait_ge(S.router_done, tr.n + 1)
                    v.tensor_scalar(sc[:, :], bank[7][:, 0:NGR + NE], pout[:, tr.b, 2:3], None, ALU.mult)\
                     .then_inc(S.sc_ready, 1)

                def groups_a():
                    dve.wait_ge(S.sc_ready, tr.n + 1)
                    if isinstance(tr.n, int) and tr.n == 0:
                        dve.wait_ge(S.attn_w_loaded, 16 * 2)
                    v.tensor_tensor(es[:, :], sc[:, NGR:NGR + NE], bias_b[:, :], ALU.add).then_inc(S.route, 1)
                    v.max(gm8[:, :], sc[:, 0:NGR]).then_inc(S.route, 1)

                def groups_b():
                    dve.wait_ge(S.route, R * tr.n + 2)
                    hold(dve)
                    v.max_index(gi8[:, :], gm8[:, :], sc[:, 0:NGR]).then_inc(S.route, 1)

                def groups_c():
                    dve.wait_ge(S.route, R * tr.n + 3)
                    v.tensor_tensor(geq[:, :, :], numbers[:, 0:NGR].unsqueeze(2).broadcast_to([P, NGR, TOPG]),
                                    gi8[:, 0:TOPG].unsqueeze(1).broadcast_to([P, NGR, TOPG]), ALU.is_equal)\
                     .then_inc(S.route, 1)

                def groups_d():
                    dve.wait_ge(S.route, R * tr.n + 4)
                    v.tensor_reduce(gsel[:, :], geq[:, :, :], AX.X, ALU.add).then_inc(S.route, 1)

                def masked_a():
                    dve.wait_ge(S.route, R * tr.n + 5)
                    v.tensor_scalar(gpen[:, :], gsel[:, :], 1e9, -1e9, ALU.mult, ALU.add).then_inc(S.route, 1)
                    v.tensor_tensor(by_group(es2[:, :]), by_group(es[:, :]),
                                    gsel[:, :].unsqueeze(2).broadcast_to([P, NGR, EPG]), ALU.mult)\
                     .then_inc(S.route, 1)

                def masked_b():
                    dve.wait_ge(S.route, R * tr.n + 7)
                    v.tensor_tensor(by_group(es[:, :]), by_group(es2[:, :]),
                                    gpen[:, :].unsqueeze(2).broadcast_to([P, NGR, EPG]), ALU.add)\
                     .then_inc(S.route, 1)

                def experts_a():
                    dve.wait_ge(S.route, R * tr.n + 8)
                    hold(dve)
                    v.max(em8[:, :], es[:, :]).then_inc(S.route, 1)

                def experts_b():
                    dve.wait_ge(S.route, R * tr.n + 9)
                    wait(dve, S.gate_exp, tr.n - 1)
                    hold(dve)
                    v.tensor_scalar(ed4[:, tr.b], em8[:, 0:TOPK], em8[:, 0:1], None, ALU.subtract)\
                     .then_inc(S.route, 1)
                    v.max_index(ei8[:, :], em8[:, :], es[:, :]).then_inc(S.route, 1)

                def marks_a():
                    dve.wait_ge(S.route, R * tr.n + 11)
                    v.tensor_tensor(oh[:, :, :], numbers.unsqueeze(1).broadcast_to([P, TOPK, NE]),
                                    ei8[:, 0:TOPK].unsqueeze(2).broadcast_to([P, TOPK, NE]), ALU.is_equal)\
                     .then_inc(S.route, 1)

                def marks_b():
                    dve.wait_ge(S.route, R * tr.n + 12)
                    wait(dve, S.pos_done, tr.n - 1)
                    with nc.allow_low_precision("marks are 0 or 1"):
                        v.tensor_reduce(msel[:, tr.b], oh[:, :, :].rearrange("p k e -> p e k"), AX.X, ALU.add)\
                         .then_inc(S.sel_ready, 1)

                def totals():
                    dve.wait_ge(S.pos_done, tr.n + 1)
                    v.tensor_tensor(macc[:, 1 - tr.b], macc[:, tr.b], msel[:, tr.b], ALU.add).then_inc(S.acc_ready, 1)

                def positions_a():
                    dve.wait_ge(S.pos_done, tr.n + 1)
                    v.tensor_tensor(ohp[:, :, :], oh[:, :, :],
                                    bank[6][:, P:P + NE].unsqueeze(1).broadcast_to([P, TOPK, NE]), ALU.mult)\
                     .then_inc(S.pos_read, 1)

                def positions_b():
                    dve.wait_ge(S.pos_read, tr.n + 1)
                    v.tensor_reduce(posk[:, :], ohp[:, :, :], AX.X, ALU.add).then_inc(S.slots, 1)

                def slots_a():
                    dve.wait_ge(S.slots, 4 * tr.n + 1)
                    v.tensor_scalar(keep[:, :], posk[:, :], float(cap), None, ALU.is_lt).then_inc(S.slots, 1)
                    v.scalar_tensor_tensor(slotf[:, :], ei8[:, 0:TOPK], float(cap), posk[:, :], ALU.mult,
                                           ALU.add).then_inc(S.slots, 1)

                def slots_b():
                    dve.wait_ge(S.slots, 4 * tr.n + 3)
                    v.scalar_tensor_tensor(slotf2[:, :], keep[:, :], -OOB, slotf[:, :], ALU.mult, ALU.add)\
                     .then_inc(S.slots, 1)

                def slots_c():
                    dve.wait_ge(S.slots, 4 * tr.n + 4)
                    wait(dve, dispatched[tr.b], 16 * TOPK * tr.half)
                    v.tensor_scalar(sidx[:, tr.b], slotf2[:, :], OOB, None, ALU.add).then_inc(S.slot_ready, 1)

                def gates_a():
                    dve.wait_ge(S.gate_exp, tr.n + 1)
                    v.reciprocal(exr[:, :], exs[:, tr.b]).then_inc(S.gate_done, 1)

                def gates_b():
                    dve.wait_ge(S.gate_done, 2 * tr.n + 1)
                    v.scalar_tensor_tensor(gates[:, bass.ds(tr.n, 1), :].rearrange("p o k -> p (o k)"), ex4[:, tr.b],
                                           exr[:, :], keep[:, :], ALU.mult, ALU.mult).then_inc(S.gate_done, 1)

                def at(tile, operation, *args):
                    if tile is not None:
                        operation(*args)

                at(tw, weight_sums)
                at(tn, first_stats)
                at(tw, over_sums)
                at(tp, earlier_keys)
                at(tn, first_mean)
                at(tr, scores)
                at(tr, groups_a)
                at(tn, first_var)
                at(tr, groups_b)
                at(tf, rotate, 0)
                at(tr, groups_c)
                at(tf, rotate, 1)
                at(tr, groups_d)
                at(tf, rotate, 2)
                at(tr, masked_a)
                at(tp, maxima, 0)
                at(tr, masked_b)
                at(tw, add_attention)
                at(tr, experts_a)
                at(tp, maxima, 1)
                at(tw, second_stats)
                at(tr, experts_b)
                at(tw, second_mean)
                at(tr, marks_a)
                at(tp, maxima, 2)
                at(tw, second_var)
                at(tr, marks_b)
                at(tw, length_a)
                at(tf, rest)
                at(tw, length_b)
                at(tf, middle, 0)
                at(tf, middle, 1)
                at(tw, length_c)
                at(tp, maxima, 3)
                at(tr, positions_a)
                at(tp, minus_hi)
                at(tr, totals)
                at(tr, positions_b)
                at(tp, minus_rest)
                at(tr, slots_a)
                at(tp, minus_mid)
                at(tr, slots_b)
                at(tp, minus_lo)
                at(tr, gates_a)
                at(tw, second_norm)
                at(tr, gates_b)
                at(tn, first_norm)
                at(tr, slots_c)
                if isinstance(tau, int) and tau == 0:
                    dve.wait_ge(S.cent_len, 3)
                    v.tensor_scalar(cent_sq[:, :], cent[:, :], cent_n[:, 2:3], None, ALU.mult).then_inc(S.cent_unit, 1)
                    dve.wait_ge(S.centT_done, 1)
                    v.tensor_copy(centT[:, :], bank[0][:, 0:NGR + NE]).then_inc(S.centT_evac, 1)

            attention_steps(dve, step)

            def shared_step(m, md):
                if m is not None:
                    for h in range(2):
                        dve.wait_ge(S.sh_act, 2 * m.n + (h + 1))
                        dve.wait_ge(S.sh_gu, 4 * m.n + (2 * h + 2))
                        v.tensor_tensor(sact[:, m.b, h], sact[:, m.b, h], bank[2 + h][:, :], ALU.mult)\
                         .then_inc(S.sh_mul, 1)
                if md is not None:
                    dve.wait_ge(S.sh_down, md.n + 1)
                    xs = x_all[:, bass.ds(4 * md.n, 4), :]
                    v.tensor_tensor(xs, xs, bank[4 + md.b][:, :].rearrange("p (t d) -> p t d", d=D), ALU.add)\
                     .then_inc(S.sh_added, 1)

            shared_steps(shared_step, 0, SHARED_EARLY)

            def combine(q, c, turn):
                dve.wait_ge(r_arrived[c], 16 * (turn + 1))
                for k in range(2):
                    for h in range(2):
                        t = 2 * q + h
                        xt = x_all[:, bass.ds(t, 1), :].rearrange("p o d -> p (o d)")
                        if k:
                            dve.wait_ge(S.comb_step, CSTEPS * q + (h + 1))
                        gk = gates[:, bass.ds(t, 1), k:k + 1].rearrange("p o k -> p (o k)")
                        v.scalar_tensor_tensor(xt, rload[:, 2 * c + h, k], gk, xt, ALU.mult, ALU.add)\
                         .then_inc(S.comb_step, 1)
                dve.wait_ge(S.comb_step, CSTEPS * q + 4)
                dve.wait_ge(S.late_sum, q + 1)
                xp = x_all[:, bass.ds(2 * q, 2), :]
                v.tensor_tensor(xp, xp, rload[:, 2 * c:2 * c + 2, 2], ALU.add).then_inc(S.comb_step, 1)

            def expert_step(en, e, ed):
                def times_up(ch):
                    for h in range(2):
                        dve.wait_ge(S.h_act, 4 * e.n + (2 * ch + h + 1))
                        dve.wait_ge(S.gu_done, 8 * e.n + (4 * ch + 2 * h + 2))
                        hs = hact[:, e.b, h, ch * CH:(ch + 1) * CH]
                        v.tensor_tensor(hs, hs, bank[4 + h][:, 0:CH], ALU.mult).then_inc(S.h_mul, 1)

                if ed is not None:
                    dve.wait_ge(S.ypair_ready, ed.n + 1)
                    wait(dve, y_sent[ed.b], 16 * ST * ed.half)
                    v.tensor_copy(yidx[:, ed.b], ypair[:, ed.b]).then_inc(S.yidx_ready, 1)
                if en is not None:
                    dve.wait_ge(xg_arrived[en.b], 16 * (en.half + 1))
                    wait(dve, S.yidx_ready, en.n - 1)
                    v.tensor_copy(ypair[:, en.b], xg[:, en.b, :, D]).then_inc(S.ypair_ready, 1)
                    wait(dve, S.gu_done, 8 * (en.n - 1))
                    hi, lo = xgT_parts[:, en.b, 0], xgT_parts[:, en.b, 1]
                    halves = ((bank[0], 0, 4 * P), (bank[1], 4 * P, cap))
                    for q, (bk, at, to) in enumerate(halves):
                        dve.wait_ge(S.xgT_done, 2 * en.n + (q + 1))
                        v.tensor_copy(hi[:, at:to], bk[:, 0:to - at]).then_inc(S.xgT_hi, 1)
                    for q, (bk, at, to) in enumerate(halves):
                        dve.wait_ge(S.xgT_hi, 2 * en.n + (q + 1))
                        v.tensor_tensor(lo[:, at:to], bk[:, 0:to - at], hi[:, at:to].bitcast(F32), ALU.subtract)\
                         .then_inc(S.xgT_lo, 1)
                if e is not None:
                    times_up(0)
                if en is not None:
                    dve.wait_ge(S.wgu_hi, en.n + 1)
                    v.tensor_tensor(wgu_parts[:, en.b, 1], wgu[:, en.b], wgu_parts[:, en.b, 0].bitcast(F32),
                                    ALU.subtract).then_inc(S.wgu_lo, 1)
                if e is not None:
                    times_up(1)

            lagged_steps(dve, expert_step, NE, True)

            def shared_and_combine(m, md):
                shared_step(m, md)
                if md is not None and md.n > SHARED_EARLY and md.n < N // 512 - 1:
                    q = 2 * (md.n - SHARED_EARLY - 1)
                    dve.wait_ge(S.sh_added, md.n)
                    combine(q, q % (NR // 2), q // (NR // 2))
                    combine(q + 1, (q + 1) % (NR // 2), (q + 1) // (NR // 2))

            shared_steps(shared_and_combine, SHARED_EARLY, N // 512)

            dve.wait_ge(S.sh_added, N // 512)
            for q in range(COMB_EARLY // 2, NR):
                combine(q, q % (NR // 2), q // (NR // 2))
            with dve.Fori(0, NT // NR - 2) as i:
                for c in range(NR // 2):
                    combine((NR // 2) * i + (NR + c), c, i + 2)


_INS = ["L0_attn_x", "L0_attn_Wqkv", "L0_attn_Wout", "L0_ffn_group_centroids", "L0_ffn_expert_centroids",
        "L0_ffn_bias", "L0_ffn_wg", "L0_ffn_wu", "L0_ffn_wd", "L0_ffn_sg", "L0_ffn_su", "L0_ffn_sd"]


def kernel(**inputs):
    import numpy as _np
    import concourse.bacc as _bacc
    from concourse import mybir as _mybir
    from concourse.bass_utils import run_bass_kernel_spmd as _run

    nc = _bacc.Bacc("TRN2", target_bir_lowering=False, num_devices=1)
    arrays, args = {}, []
    for name in _INS:
        a = _np.ascontiguousarray(inputs[name])
        arrays[f"in_{name}_dram"] = a
        args.append(nc.dram_tensor(f"in_{name}_dram", a.shape, _mybir.dt.from_np(a.dtype), kind="ExternalInput").ap())
    shape = inputs["L0_attn_x"].shape
    const, where, cap = constants(shape[0] * shape[1], shape[1])
    arrays["constants_dram"] = const
    args.append(nc.dram_tensor("constants_dram", const.shape, _mybir.dt.float32, kind="ExternalInput").ap())
    args.append(nc.dram_tensor("out_0_dram", shape, _mybir.dt.float32, kind="ExternalOutput").ap())
    block_kernel(nc, *args, where, cap)
    r = _run(nc, [arrays], core_ids=[0])
    return r.results[0]["out_0_dram"]
```
